# Optimizing a Trainium2 kernel written in Bass

```python
import numpy as np
import jax
import jax.numpy as jnp

def _softmax(x, axis=-1):
    return jax.nn.softmax(x, axis=axis)

def _gelu(x):
    return jax.nn.gelu(x, approximate=True)

def _silu(x):
    return jax.nn.silu(x)

def _sigmoid(x):
    return jax.nn.sigmoid(x)

def _layernorm(x, axis=-1, eps=1e-05):
    m = jnp.mean(x, axis=axis, keepdims=True)
    v = jnp.var(x, axis=axis, keepdims=True)
    return (x - m) / jnp.sqrt(v + eps)

def _scatter_add(tgt, idx, src, axis=0):
    return tgt.at[idx].add(src)

def _segment_sum(src, seg, n):
    return jax.ops.segment_sum(src, seg, n)
kernel_name = 'mk_macaron_d1_jaxref_r4_3b79d4'

def setup_inputs(seed: int=0):
    np.random.seed(seed)
    _w = jnp.asarray

    def _L0_attn_setup():
        import jax, jax.numpy as jnp
        import numpy as np
        from jax import lax
        B, T, HID, NH = (4, 512, 256, 16)
        D = HID // NH
        LN_EPS = 1e-05
        NORM_EPS = 1e-06
        key = jax.random.key(seed)
        ks = jax.random.split(key, 3)
        s = 0.02
        return {'x': jax.random.normal(ks[0], (B, T, HID), jnp.float32), 'ln_g': jnp.ones((HID,), jnp.float32), 'ln_b': jnp.zeros((HID,), jnp.float32), 'w_qkvb': jax.random.normal(ks[1], (HID, 4 * HID), jnp.float32) * s, 'b_qkvb': jnp.zeros((4 * HID,), jnp.float32), 'w_out': jax.random.normal(ks[2], (HID, HID), jnp.float32) * s, 'b_out': jnp.zeros((HID,), jnp.float32)}
    _L0_attn_in = _L0_attn_setup()

    def _L0_ffn_setup():
        import jax, jax.numpy as jnp
        import numpy as np
        D_IN, D_HID = (256, 1024)

        def _ternary(key, shape):
            return jax.random.randint(key, shape, -1, 2).astype(jnp.float32)

        def _tlin(x, w, s):
            return jnp.einsum('bsi,oi->bso', x, w) * s
        key = jax.random.key(seed)
        ks = jax.random.split(key, 12)
        inv = lambda fan: 1.0 / np.sqrt(fan).astype(np.float32)
        return {'x': jax.random.normal(ks[0], (4, 512, D_IN), dtype=jnp.float32), 'w1_w': _ternary(ks[1], (D_HID, D_IN)), 'w1_s': jax.random.uniform(ks[2], (D_HID,), dtype=jnp.float32) * inv(D_IN), 'w2_w': _ternary(ks[3], (D_HID, D_IN)), 'w2_s': jax.random.uniform(ks[4], (D_HID,), dtype=jnp.float32) * inv(D_IN), 'h1_w': _ternary(ks[5], (D_HID, D_HID)), 'h1_s': jax.random.uniform(ks[6], (D_HID,), dtype=jnp.float32) * inv(D_HID), 'h2_w': _ternary(ks[7], (D_HID, D_HID)), 'h2_s': jax.random.uniform(ks[8], (D_HID,), dtype=jnp.float32) * inv(D_HID), 'w3_w': _ternary(ks[9], (D_IN, D_HID)), 'w3_s': jax.random.uniform(ks[10], (D_IN,), dtype=jnp.float32) * inv(D_HID)}
    _L0_ffn_in = _L0_ffn_setup()
    _d = {'L0_attn_x': _L0_attn_in['x'], 'L0_attn_ln_g': _L0_attn_in['ln_g'], 'L0_attn_ln_b': _L0_attn_in['ln_b'], 'L0_attn_w_qkvb': _L0_attn_in['w_qkvb'], 'L0_attn_b_qkvb': _L0_attn_in['b_qkvb'], 'L0_attn_w_out': _L0_attn_in['w_out'], 'L0_attn_b_out': _L0_attn_in['b_out'], 'L0_ffn_w1_w': _L0_ffn_in['w1_w'], 'L0_ffn_w1_s': _L0_ffn_in['w1_s'], 'L0_ffn_w2_w': _L0_ffn_in['w2_w'], 'L0_ffn_w2_s': _L0_ffn_in['w2_s'], 'L0_ffn_h1_w': _L0_ffn_in['h1_w'], 'L0_ffn_h1_s': _L0_ffn_in['h1_s'], 'L0_ffn_h2_w': _L0_ffn_in['h2_w'], 'L0_ffn_h2_s': _L0_ffn_in['h2_s'], 'L0_ffn_w3_w': _L0_ffn_in['w3_w'], 'L0_ffn_w3_s': _L0_ffn_in['w3_s']}
    _x0 = _d['L0_attn_x']
    _d['L0_attn_x'] = jax.random.normal(jax.random.fold_in(jax.random.key(seed), 1), (4, 1024, 256), dtype=_x0.dtype)
    del _x0
    return _d

def reference(L0_attn_x, L0_attn_ln_g, L0_attn_ln_b, L0_attn_w_qkvb, L0_attn_b_qkvb, L0_attn_w_out, L0_attn_b_out, L0_ffn_w1_w, L0_ffn_w1_s, L0_ffn_w2_w, L0_ffn_w2_s, L0_ffn_h1_w, L0_ffn_h1_s, L0_ffn_h2_w, L0_ffn_h2_s, L0_ffn_w3_w, L0_ffn_w3_s):

    def _L0_attn_ref(x, ln_g, ln_b, w_qkvb, b_qkvb, w_out, b_out):
        import jax, jax.numpy as jnp
        import numpy as np
        from jax import lax
        B, T, HID, NH = (4, 512, 256, 16)
        D = HID // NH
        LN_EPS = 1e-05
        NORM_EPS = 1e-06
        b, t = x.shape[:2]
        mu = jnp.mean(x, axis=-1, keepdims=True)
        var = jnp.mean((x - mu) ** 2, axis=-1, keepdims=True)
        normed = (x - mu) * lax.rsqrt(var + LN_EPS) * ln_g + ln_b
        proj = normed @ w_qkvb + b_qkvb
        q, k, v, beta_pre = jnp.split(proj, 4, axis=-1)
        beta = jax.nn.sigmoid(beta_pre)

        def heads(a):
            return a.reshape(b, t, NH, D).transpose(1, 0, 2, 3)
        q, k, v, beta = (heads(q), heads(k), heads(v), heads(beta))
        k = k / jnp.maximum(jnp.linalg.norm(k, axis=-1, keepdims=True), NORM_EPS)
        S0 = jnp.zeros((b, NH, D, D), x.dtype)

        def step(S, inp):
            q_t, k_t, v_t, beta_t = inp
            retrieval = jnp.einsum('bhij,bhj->bhi', S, k_t)
            S = S + jnp.einsum('bhi,bhj->bhij', beta_t * (v_t - retrieval), k_t)
            o_t = jnp.einsum('bhij,bhj->bhi', S, q_t)
            return (S, o_t)
        _, out_t = lax.scan(step, S0, (q, k, v, beta))
        scan_out = out_t.transpose(1, 0, 2, 3).reshape(b, t, NH * D)
        return x + scan_out @ w_out + b_out

    def _L0_ffn_ref(x, w1_w, w1_s, w2_w, w2_s, h1_w, h1_s, h2_w, h2_s, w3_w, w3_s):
        import jax, jax.numpy as jnp
        import numpy as np
        D_IN, D_HID = (256, 1024)

        def _ternary(key, shape):
            return jax.random.randint(key, shape, -1, 2).astype(jnp.float32)

        def _tlin(x, w, s):
            return jnp.einsum('bsi,oi->bso', x, w) * s
        h = jax.nn.silu(_tlin(x, w1_w, w1_s)) * _tlin(x, w2_w, w2_s)
        h = jax.nn.gelu(_tlin(h, h1_w, h1_s), approximate=False)
        h = jax.nn.gelu(_tlin(h, h2_w, h2_s), approximate=False)
        return _tlin(h, w3_w, w3_s)
    x = L0_attn_x
    x = x + 0.5 * _L0_ffn_ref(_layernorm(x, axis=-1), L0_ffn_w1_w, L0_ffn_w1_s, L0_ffn_w2_w, L0_ffn_w2_s, L0_ffn_h1_w, L0_ffn_h1_s, L0_ffn_h2_w, L0_ffn_h2_s, L0_ffn_w3_w, L0_ffn_w3_s)
    x = x + _L0_attn_ref(_layernorm(x, axis=-1), L0_attn_ln_g, L0_attn_ln_b, L0_attn_w_qkvb, L0_attn_b_qkvb, L0_attn_w_out, L0_attn_b_out)
    x = x + 0.5 * _L0_ffn_ref(_layernorm(x, axis=-1), L0_ffn_w1_w, L0_ffn_w1_s, L0_ffn_w2_w, L0_ffn_w2_s, L0_ffn_h1_w, L0_ffn_h1_s, L0_ffn_h2_w, L0_ffn_h2_s, L0_ffn_w3_w, L0_ffn_w3_s)
    return x

_drawn_inputs = setup_inputs


def setup_inputs(seed=0):
    import zlib

    import numpy as np

    out = dict(_drawn_inputs(seed))
    spreads = {'L0_attn_ln_g': (1.0, 0.2),
     'L0_attn_ln_b': (0.0, 0.1),
     'L0_attn_b_qkvb': (0.0, 0.1),
     'L0_attn_b_out': (0.0, 0.1)}
    factors = {}
    for name, (base, spread) in spreads.items():
        noise = np.random.default_rng([zlib.crc32(name.encode()), seed]).standard_normal(out[name].shape)
        drawn = base * np.exp(spread * noise) if base else spread * noise
        out[name] = jnp.asarray(drawn.astype(out[name].dtype))
    for name, factor in factors.items():
        out[name] = (out[name] * factor).astype(out[name].dtype)
    return out
```

```python
from contextlib import ExitStack

import concourse.bass as bass
from concourse import mybir

F32 = mybir.dt.float32
F16 = mybir.dt.float16
ALU = mybir.AluOpType
ACT = mybir.ActivationFunctionType
AX = mybir.AxisListType

P = 128
B, T, HID = 4, 1024, 256
NH, D = 16, 16
FF = 1024
LN_EPS = 1e-5
NORM_EPS = 1e-6

KT_IN = HID // P
KT_FF = FF // P
SLAB_T = 128
SLABS = T // SLAB_T
N = B * SLAB_T
C = 16
CH = SLAB_T // C
HP = P // D
GB = KT_IN * B
ITEMS = KT_IN * 2 * CH
RUNS = 2 * ITEMS
COLS = KT_IN * N

PAR = {}
for _name, _n in (("w1_s", KT_FF), ("w2_s", KT_FF), ("h1_s", KT_FF), ("h2_s", KT_FF), ("w3_s", KT_IN),
                  ("ln_g", KT_IN), ("ln_b", KT_IN), ("b_qkvb", 4 * KT_IN), ("b_out", KT_IN)):
    PAR[_name] = (sum(n for _, n in PAR.values()), _n)
NPAR = sum(n for _, n in PAR.values())


HALVES = 2
HCH = CH // HALVES
HRUNS = RUNS // HALVES

KK = [(t, t) for t in range(1, C)]
QK = []
for _t in range(C):
    _h = 1 if RUNS * (_t + 1) <= 512 else 2
    QK += [(_t, _t + 1, RUNS // _h * _i, RUNS // _h) for _i in range(_h)]
KK_AT = [HRUNS * t * (t - 1) // 2 for t in range(C + 1)]

RING = 4
FFN_BANKS = 4
FFN_USES = "VV" + "SV" * KT_FF + "S" * (2 * KT_FF) + "V" * KT_IN
ATT_BANKS = 3
ATT_USES = "VV" + "S" * (4 * KT_IN) + "V" * KT_IN + "V" * (HALVES * len(KK)) + "V" * len(QK) + "V" * KT_IN
U_PROJ = 2
U_NORM = U_PROJ + 4 * KT_IN
U_KK = U_NORM + KT_IN
U_QK = U_KK + HALVES * len(KK)
U_OUT = U_QK + len(QK)


def reads(uses, who, j):
    return uses[:j + 1].count(who)


FV, FS = FFN_USES.count("V"), FFN_USES.count("S")
AV, AS = ATT_USES.count("V"), ATT_USES.count("S")
UNITS = 3 * KT_FF


STEP_ROOTS = 2
STEP_NORMED = STEP_ROOTS + 1
STEP_KNORM = STEP_NORMED + 1
CHUNK_STEPS = 2 + 2 * (C - 1) + 1
STEP_CHUNKS = STEP_KNORM
STEP_O = STEP_CHUNKS + CH * CHUNK_STEPS
ATT_STEPS = STEP_O + 1


def build(nc, x, w1, w2, h1, h2, w3, wqkvb, wout, par, out):
    with ExitStack() as ctx:
        def sb(name, shape, dt=F32):
            return ctx.enter_context(nc.sbuf_tensor(name, shape, dt))

        def bank(name):
            return ctx.enter_context(nc.psum_tensor(name, [P, 512], F32))

        def sem(name):
            return ctx.enter_context(nc.semaphore(name))

        w1_sb = sb("w1_sb", [P, KT_IN, FF], F16)
        w2_sb = sb("w2_sb", [P, KT_IN, FF], F16)
        h1_sb = sb("h1_sb", [P, KT_FF, FF], F16)
        h2_sb = sb("h2_sb", [P, KT_FF, FF], F16)
        w3_sb = sb("w3_sb", [P, KT_FF, HID], F16)
        wqkvb_sb = sb("wqkvb_sb", [P, KT_IN, 4 * HID])
        wout_sb = sb("wout_sb", [P, KT_IN, HID])
        par_sb = sb("par_sb", [P, NPAR])
        w3_half = sb("w3_half", [P, KT_IN])
        ln_gain = sb("ln_gain", [P, KT_IN])
        average = sb("average", [P, P])
        head_ones = sb("head_ones", [P, P])
        head_minus = sb("head_minus", [P, P])
        X = sb("X", [P, RING, KT_IN, N])
        xc = sb("xc", [P, KT_IN, N])
        xsq = sb("xsq", [P, KT_IN, N])
        rstd = sb("rstd", [P, 2, N])
        xn = xsq
        xn_hi = sb("xn_hi", [P, KT_IN, N], F16)
        xn_lo = sb("xn_lo", [P, KT_IN, N], F16)
        gate = sb("gate", [P, 2, N])
        hid = sb("hid", [P, 3, N])
        hid_hi = [sb(f"hid_hi{i}", [P, KT_FF, N], F16) for i in range(2)]
        hid_lo = [sb(f"hid_lo{i}", [P, KT_FF, N], F16) for i in range(2)]
        KQ = sb("KQ", [P, 2, COLS])
        V = sb("V", [P, COLS])
        beta = sb("beta", [P, COLS])
        U = sb("U", [P, COLS])
        O = sb("O", [P, COLS])
        O_in = sb("O_in", [P, COLS])
        k_sq = sb("k_sq", [P, COLS])
        NK = sb("NK", [P, KK_AT[C]])
        pairs = sb("pairs", [P, 3, 512])
        qk_u = sb("qk_u", [P, 2, 512])
        KTr = sb("KTr", [P, ITEMS, 32])
        Kz = sb("Kz", [P, 2, GB, P])
        UTr = sb("UTr", [P, GB // 2, 32])
        terms = sb("terms", [P, C, GB, C])
        resid = sb("resid", [P, GB, C])
        state = sb("state", [P, GB, 32])
        state_bd = sb("state_bd", [P, GB, P])

        ffn_bank = [bank(f"ffn_bank{i}") for i in range(FFN_BANKS)]
        att_bank = [bank(f"att_bank{i}") for i in range(ATT_BANKS)]
        state_bank = bank("state_bank")
        retr_ps = state_bank[:, 0:GB * 2 * C]
        dstate_ps = state_bank[:, 256:512]

        x_loaded, par_loaded, att_w_loaded = sem("x_loaded"), sem("par_loaded"), sem("att_w_loaded")
        w12_loaded, h1_loaded, h2_loaded, w3_loaded = (sem(n) for n in ("w12_loaded", "h1_loaded", "h2_loaded", "w3_loaded"))
        stored = sem("stored")
        masks_step, masks_ready, consts_ready, state_zeroed = (sem(n) for n in ("masks_step", "masks_ready", "consts_ready", "state_zeroed"))
        ffn_filled, ffn_read_v, ffn_read_s = sem("ffn_filled"), sem("ffn_read_v"), sem("ffn_read_s")
        ffn_squared, ffn_normed, ffn_rooted = sem("ffn_squared"), sem("ffn_normed"), sem("ffn_rooted")
        ffn_hi, ffn_lo, hid_hi_ready, hid_lo_ready = (sem(n) for n in ("ffn_hi", "ffn_lo", "hid_hi_ready", "hid_lo_ready"))
        ffn_step = sem("ffn_step")
        att_filled, att_read_v, att_read_s = sem("att_filled"), sem("att_read_v"), sem("att_read_s")
        att_squared, att_rooted, att_normed, att_scaled = (sem(n) for n in ("att_squared", "att_rooted", "att_normed", "att_scaled"))
        y_added, k_ready, k_turned = sem("y_added"), sem("k_ready"), sem("k_turned")
        pairs_ready, kz_ready = sem("pairs_ready"), sem("kz_ready")
        retr_ready, resid_ready, q_saved = sem("retr_ready"), sem("resid_ready"), sem("q_saved")
        u_turned, dstate_ready, state_ready = sem("u_turned"), sem("dstate_ready"), sem("state_ready")
        att_step, o_ready = sem("att_step"), sem("o_ready")

        def p(name, j):
            a = PAR[name][0] + j
            return par_sb[:, a:a + 1]

        def slab(s):
            return X[:, bass.ds(s % RING, 1), :, :].rearrange("p s k n -> p (s k) n")

        def runs(ap):
            return ap.rearrange("p (r t) -> p r t", t=C)

        def at_chunk(ap, c):
            return ap.rearrange("p (g c b t) -> p g c b t", c=CH, b=2, t=C)[:, :, c, :, :]

        def nk_row(t, c):
            row = NK[:, KK_AT[t]:KK_AT[t + 1]]
            return row.rearrange("p (g c b t) -> p g c b t", c=HCH, b=2, t=t)[:, :, c % HCH, :, :]

        def half(ap, h):
            view = ap.rearrange("p (g h r t) -> p g h r t", h=HALVES, r=2 * HCH, t=C)
            return view[:, :, h, :, :]

        def four(ap):
            return ap.rearrange("p (g b) t -> p g b t", b=2)

        FFN_U = len(FFN_USES)
        ATT_U = len(ATT_USES)

        block = ctx.enter_context(nc.Block())

        @block.sync
        def _(sp):
            sp.dma_start(par_sb[:, :], par).then_inc(par_loaded, 16)
            def load(s, slot):
                sp.dma_start(X[:, bass.ds(slot, 1), :, :], x[:, bass.ds(s, 1), :, :]).then_inc(x_loaded, 16)

            def store(s, slot):
                sp.wait_ge(ffn_read_v, (s * 2 + 2) * FV)
                sp.dma_start(out[:, bass.ds(s, 1), :, :], X[:, bass.ds(slot, 1), :, :]).then_inc(stored, 16)

            load(0, 0)
            sp.dma_start(wqkvb_sb[:, :, :], wqkvb).then_inc(att_w_loaded, 16)
            sp.dma_start(wout_sb[:, :, :], wout).then_inc(att_w_loaded, 16)
            sp.wait_ge(x_loaded, 16)
            load(1, 1)
            with sp.Fori(0, SLABS - 2) as s:
                slot, next_slot = sp.snap(s % RING), sp.snap((s + 2) % RING)
                store(s, slot)
                sp.wait_ge(stored, (s + 1) * 16)
                sp.wait_ge(x_loaded, s * 16 + 32)
                load(s + 2, next_slot)
            for s in (SLABS - 2, SLABS - 1):
                store(s, s % RING)
            sp.wait_ge(stored, 16 * SLABS)

        @block.gpsimd
        def _(pool):
            pool.dma_start(w1_sb[:, :, :], w1).then_inc(w12_loaded, 16)
            pool.dma_start(w2_sb[:, :, :], w2).then_inc(w12_loaded, 16)
            pool.dma_start(h1_sb[:, :, :], h1).then_inc(h1_loaded, 16)
            pool.dma_start(h2_sb[:, :, :], h2).then_inc(h2_loaded, 16)
            pool.dma_start(w3_sb[:, :, :], w3).then_inc(w3_loaded, 16)
            pool.memset(average[:, :], 1.0 / HID).then_inc(masks_ready, 1)
            for n, (m, v) in enumerate(((head_ones, 1.0), (head_minus, -1.0))):
                pool.memset(m[:, :], v).then_inc(masks_step, 1)
                pool.wait_ge(masks_step, 2 * n + 1)
                view = m[:, :].rearrange("p (h i) -> p h i", i=D)
                pool.affine_select(out=view, in_=view, compare_op=ALU.is_ge, fill=0.0, base=0,
                                   pattern=[[-D, HP], [0, D]], channel_multiplier=1).then_inc(masks_step, 1)
                pool.wait_ge(masks_step, 2 * n + 2)
                pool.affine_select(out=view, in_=view, compare_op=ALU.is_ge, fill=0.0, base=D - 1,
                                   pattern=[[D, HP], [0, D]], channel_multiplier=-1).then_inc(masks_ready, 1)
            pool.memset(state[:, :, :], 0.0).then_inc(state_zeroed, 1)
            pool.memset(state_bd[:, :, :], 0.0).then_inc(state_ready, 1)
            pool.wait_ge(masks_ready, 3)

            def ffn(n):
                pool.wait_ge(ffn_hi, n * 1 + 1)
                pool.tensor_tensor(xn_lo[:, :, :], xn[:, :, :], xn_hi[:, :, :], ALU.subtract).then_inc(ffn_lo, 1)
                for u in range(UNITS):
                    layer, m = divmod(u, KT_FF)
                    pool.wait_ge(hid_hi_ready, n * UNITS + (u + 1))
                    pool.tensor_tensor(hid_lo[layer % 2][:, m, :], hid[:, u % 3, :], hid_hi[layer % 2][:, m, :],
                                       ALU.subtract).then_inc(hid_lo_ready, 1)

            def pair_buffer(s, q):
                if q >= 3:
                    pool.wait_ge(att_filled, s * ATT_U + (U_KK + q - 3 + 1))
                return pairs[:, q % 3, :]

            def make_kk(s, h):
                keys = half(KQ[:, 0, :], h)
                for j, (t, w) in enumerate(KK):
                    o = pair_buffer(s, h * len(KK) + j)[:, 0:HRUNS * w].rearrange("p (g r w) -> p g r w", g=GB // 2, w=w)
                    pool.tensor_tensor(o, keys[:, :, :, t:t + 1].to_broadcast([P, GB // 2, 2 * HCH, w]), keys[:, :, :, 0:w],
                                       ALU.mult).then_inc(pairs_ready, 1)

            def make_qk(s):
                for j, (t, w, r0, nr) in enumerate(QK):
                    o = pair_buffer(s, HALVES * len(KK) + j)[:, 0:nr * w].rearrange("p (r w) -> p r w", w=w)
                    pool.tensor_tensor(o, runs(KQ[:, 1, :])[:, r0:r0 + nr, t:t + 1].to_broadcast([P, nr, w]),
                                       runs(KQ[:, 0, :])[:, r0:r0 + nr, 0:w], ALU.mult).then_inc(pairs_ready, 1)

            def kz(s, c):
                if c >= 2:
                    pool.wait_ge(dstate_ready, s * CH + (c - 1))
                for b in range(2):
                    o = Kz[:, c % 2, :, :].rearrange("p (g b) (q w) -> p g b q w", b=2, w=32)[:, :, b, :, :]
                    keys = KTr[:, :, :].rearrange("p (g c) w -> p g c w", c=CH)[:, :, c:c + 1, :]
                    mask = head_ones[:, :].rearrange("p (q b w) -> p b q w", b=2, w=D)[:, b, :, 0:1]
                    pool.tensor_tensor(o, keys.to_broadcast([P, GB // 2, P // 32, 32]),
                                       mask.rearrange("p q w -> p (q w)").unsqueeze(1).unsqueeze(3).to_broadcast([P, GB // 2, P // 32, 32]),
                                       ALU.mult).then_inc(kz_ready, 1)

            def attention(s):
                pool.wait_ge(att_rooted, s * 2 + 1)
                xs = slab(s)
                pool.tensor_tensor(O[:, :].rearrange("p (k n) -> p k n", k=KT_IN), xc[:, :, :],
                                   rstd[:, 0:1, :].to_broadcast([P, KT_IN, N]), ALU.mult).then_inc(att_scaled, 1)
                pool.wait_ge(att_scaled, s * 1 + 1)
                pool.tensor_tensor(xs, xs, O[:, :].rearrange("p (k n) -> p k n", k=KT_IN), ALU.add).then_inc(y_added, 1)
                pool.wait_ge(k_ready, s * KT_IN + KT_IN)
                pool.wait_ge(k_turned, s * 1 + 1)
                for h in range(HALVES):
                    make_kk(s, h)
                    for c in range(h * HCH, (h + 1) * HCH):
                        kz(s, c)
                make_qk(s)

            with pool.Fori(0, SLABS) as s:
                ffn(s * 2)
                attention(s)
                ffn(s * 2 + 1)

        @block.scalar
        def _(act):
            act.wait_ge(par_loaded, 16)
            act.mul(w3_half[:, :], par_sb[:, PAR["w3_s"][0]:PAR["w3_s"][0] + KT_IN], 0.5).then_inc(consts_ready, 1)
            act.mul(ln_gain[:, :], par_sb[:, PAR["ln_g"][0]:PAR["ln_g"][0] + KT_IN],
                    (1.0 + LN_EPS) ** -0.5).then_inc(consts_ready, 1)
            act.wait_ge(consts_ready, 2)

            def ffn(n):
                act.wait_ge(ffn_read_v, n * FV + 1)
                act.activation(xsq[:, :, :], xc[:, :, :], ACT.Square).then_inc(ffn_squared, 1)
                act.wait_ge(ffn_step, n * 2 + 2)
                act.activation(rstd[:, 0, :], rstd[:, 0, :], ACT.Sqrt).then_inc(ffn_rooted, 1)
                act.wait_ge(ffn_normed, n * 1 + 1)
                act.copy(xn_hi[:, :, :], xn[:, :, :]).then_inc(ffn_hi, 1)

                def high(u):
                    layer, m = divmod(u, KT_FF)
                    act.copy(hid_hi[layer % 2][:, m, :], hid[:, u % 3, :]).then_inc(hid_hi_ready, 1)

                for m in range(KT_FF):
                    j = 2 + 2 * m
                    act.wait_ge(ffn_filled, n * FFN_U + j + 1)
                    if m >= 2:
                        act.wait_ge(ffn_read_v, n * FV + reads(FFN_USES, "V", j - 3))
                    act.activation(gate[:, m % 2, :], ffn_bank[j % FFN_BANKS][:, :], ACT.Silu,
                                   scale=p("w1_s", m)).then_inc(ffn_read_s, 1)
                    if m >= 1:
                        act.wait_ge(ffn_read_v, n * FV + reads(FFN_USES, "V", j - 1))
                        high(m - 1)
                act.wait_ge(ffn_read_v, n * FV + reads(FFN_USES, "V", 1 + 2 * KT_FF))
                high(KT_FF - 1)
                for u in range(KT_FF, UNITS):
                    layer, m = divmod(u, KT_FF)
                    j = 2 + 2 * KT_FF + u - KT_FF
                    act.wait_ge(ffn_filled, n * FFN_U + j + 1)
                    act.wait_ge(hid_lo_ready, n * UNITS + (u - 2))
                    act.activation(hid[:, u % 3, :], ffn_bank[j % FFN_BANKS][:, :], ACT.Gelu,
                                   scale=p(("h1_s", "h2_s")[layer - 1], m)).then_inc(ffn_read_s, 1)
                    act.wait_ge(ffn_read_s, n * FS + reads(FFN_USES, "S", j))
                    high(u)

            def attention(s):
                act.wait_ge(att_read_v, s * AV + 1)
                act.activation(xsq[:, :, :], xc[:, :, :], ACT.Square).then_inc(att_squared, 1)
                act.wait_ge(att_step, s * ATT_STEPS + STEP_ROOTS)
                act.activation(rstd[:, :, :], rstd[:, :, :], ACT.Sqrt).then_inc(att_rooted, 1)
                act.wait_ge(att_step, s * ATT_STEPS + STEP_NORMED)
                for k in range(KT_IN):
                    act.activation(xsq[:, k, :], xsq[:, k, :], ACT.Identity, scale=ln_gain[:, k:k + 1],
                                   bias=p("ln_b", k)).then_inc(att_normed, 1)
                dest = [KQ[:, 1, :], O_in[:, :], V[:, :], beta[:, :]]
                for j in range(4 * KT_IN):
                    which, g = divmod(j, KT_IN)
                    ps = att_bank[(U_PROJ + j) % ATT_BANKS][:, :]
                    d = dest[which][:, g * N:(g + 1) * N]
                    act.wait_ge(att_filled, s * ATT_U + U_PROJ + j + 1)
                    if which == 1:
                        act.activation(k_sq[:, g * N:(g + 1) * N], ps, ACT.Square, bias=p("b_qkvb", j))
                    act.activation(d, ps, ACT.Sigmoid if which == 3 else ACT.Identity,
                                   bias=p("b_qkvb", j)).then_inc(att_read_s, 1)
                act.wait_ge(att_step, s * ATT_STEPS + STEP_KNORM)
                act.activation(k_sq[:, :], k_sq[:, :], ACT.Sqrt).then_inc(att_rooted, 1)
                for c in range(CH):
                    act.wait_ge(resid_ready, s * CH + c + 1)
                    act.copy(at_chunk(O[:, :], c), four(retr_ps.rearrange("p (g w) -> p g w", w=2 * C)[:, :, C:2 * C])).then_inc(q_saved, 1)

            with act.Fori(0, SLABS) as s:
                ffn(s * 2)
                attention(s)
                ffn(s * 2 + 1)

        @block.vector
        def _(dve):
            dve.wait_ge(consts_ready, 2)
            dve.wait_ge(state_zeroed, 1)

            def center(xs, ps):
                return nc.vector.tensor_tensor(xc[:, :, :], xs, ps[:, :].unsqueeze(1).to_broadcast([P, KT_IN, N]), ALU.subtract)

            def ffn(n, s):
                xs = slab(s)
                dve.wait_ge(ffn_filled, n * FFN_U + 1)
                center(xs, ffn_bank[0]).then_inc(ffn_read_v, 1)
                dve.wait_ge(ffn_filled, n * FFN_U + 2)
                nc.vector.tensor_scalar(rstd[:, 0, :], ffn_bank[1][:, :], LN_EPS, None, ALU.add).then_inc(ffn_read_v, 1)
                dve.wait_ge(ffn_read_v, n * FV + 2)
                nc.vector.reciprocal(rstd[:, 0, :], rstd[:, 0, :]).then_inc(ffn_step, 2)
                dve.wait_ge(ffn_rooted, n * 1 + 1)
                nc.vector.tensor_tensor(xn[:, :, :], xc[:, :, :], rstd[:, 0:1, :].to_broadcast([P, KT_IN, N]), ALU.mult).then_inc(ffn_normed, 1)
                for m in range(KT_FF):
                    j = 3 + 2 * m
                    dve.wait_ge(ffn_filled, n * FFN_U + j + 1)
                    dve.wait_ge(ffn_read_s, n * FS + m + 1)
                    if m >= 3:
                        dve.wait_ge(hid_lo_ready, n * UNITS + m - 2)
                    nc.vector.scalar_tensor_tensor(hid[:, m % 3, :], ffn_bank[j % FFN_BANKS][:, :], p("w2_s", m),
                                                   gate[:, m % 2, :], ALU.mult, ALU.mult).then_inc(ffn_read_v, 1)
                for m in range(KT_IN):
                    j = len(FFN_USES) - KT_IN + m
                    dve.wait_ge(ffn_filled, n * FFN_U + j + 1)
                    nc.vector.scalar_tensor_tensor(xs[:, m, :], ffn_bank[j % FFN_BANKS][:, :], w3_half[:, m:m + 1],
                                                   xs[:, m, :], ALU.mult, ALU.add).then_inc(ffn_read_v, 1)

            def attention(s):
                count = [0]

                def step(ins):
                    count[0] += 1
                    ins.then_inc(att_step, 1)

                def last_step():
                    dve.wait_ge(att_step, s * ATT_STEPS + count[0])

                def use(j):
                    dve.wait_ge(att_filled, s * ATT_U + j + 1)
                    return att_bank[j % ATT_BANKS]

                xs = slab(s)
                center(xs, use(0)).then_inc(att_read_v, 1)
                var = use(1)
                step(nc.vector.tensor_scalar(rstd[:, 0, :], var[:, :], LN_EPS, None, ALU.add))
                nc.vector.tensor_scalar(rstd[:, 1, :], var[:, :], LN_EPS * LN_EPS / (1 + LN_EPS), None, ALU.add).then_inc(att_read_v, 1)
                last_step()
                dve.wait_ge(att_read_v, s * AV + 2)
                step(nc.vector.reciprocal(rstd[:, :, :], rstd[:, :, :]))
                dve.wait_ge(att_rooted, s * 2 + 1)
                step(nc.vector.tensor_tensor(xsq[:, :, :], xc[:, :, :], rstd[:, 1:2, :].to_broadcast([P, KT_IN, N]), ALU.mult))
                for g in range(KT_IN):
                    ps = use(U_NORM + g)
                    nc.vector.tensor_scalar(k_sq[:, g * N:(g + 1) * N], ps[:, :], NORM_EPS * NORM_EPS, None, ALU.max).then_inc(att_read_v, 1)
                dve.wait_ge(att_read_v, s * AV + reads(ATT_USES, "V", U_KK - 1))
                step(nc.vector.reciprocal(k_sq[:, :], k_sq[:, :]))
                assert count[0] == STEP_KNORM
                dve.wait_ge(att_rooted, s * 2 + 2)
                for g in range(KT_IN):
                    cols = slice(g * N, (g + 1) * N)
                    nc.vector.tensor_tensor(KQ[:, 0, cols], O_in[:, cols], k_sq[:, cols], ALU.mult).then_inc(k_ready, 1)
                dve.wait_ge(k_ready, s * KT_IN + KT_IN)
                nc.vector.transpose(KTr[:, :, :].rearrange("p i w -> p (i w)"), KQ[:, 0, :]).then_inc(k_turned, 1)
                def take_kk(h):
                    for j, (t, w) in enumerate(KK):
                        ps = use(U_KK + h * len(KK) + j)
                        o = NK[:, KK_AT[t]:KK_AT[t + 1]].rearrange("p (g r w) -> p g r w", g=GB // 2, w=w)
                        nc.vector.tensor_tensor(o, ps[:, 0:HRUNS * w].rearrange("p (g r w) -> p g r w", g=GB // 2, w=w),
                                                half(beta[:, :], h)[:, :, :, t:t + 1].to_broadcast([P, GB // 2, 2 * HCH, w]),
                                                ALU.mult).then_inc(att_read_v, 1)
                    dve.wait_ge(att_read_v, s * AV + reads(ATT_USES, "V", U_KK + (h + 1) * len(KK) - 1))

                for c in range(CH):
                    if c % HCH == 0:
                        take_kk(c // HCH)
                    dve.wait_ge(retr_ready, s * CH + c + 1)
                    retr = retr_ps.rearrange("p (g w) -> p g w", w=2 * C)[:, :, 0:C]
                    nc.vector.tensor_tensor(four(resid[:, :, :]), at_chunk(V[:, :], c), four(retr), ALU.subtract).then_inc(resid_ready, 1)
                    dve.wait_ge(resid_ready, s * CH + c + 1)
                    heads = terms[:, :, :, 0].rearrange("p t g -> p g t")
                    step(nc.vector.tensor_tensor(four(heads), four(resid[:, :, :]), at_chunk(beta[:, :], c), ALU.mult))
                    u = at_chunk(U[:, :], c)
                    last_step()
                    step(nc.vector.tensor_copy(u[:, :, :, 0], four(terms[:, 0, :, 0:1])[:, :, :, 0]))
                    for t in range(1, C):
                        last_step()
                        step(nc.vector.tensor_tensor(four(terms[:, t, :, 1:t + 1]), nk_row(t, c), u[:, :, :, 0:t], ALU.mult))
                        last_step()
                        step(nc.vector.tensor_reduce(u[:, :, :, t], four(terms[:, t, :, 0:t + 1]), AX.X, ALU.add))
                    last_step()
                    nc.vector.transpose(UTr[:, :, :], u.rearrange("p g b t -> p g (b t)")).then_inc(u_turned, 1)
                    dve.wait_ge(dstate_ready, s * CH + c + 1)
                    step(nc.vector.tensor_tensor(state[:, :, :], state[:, :, :], dstate_ps.rearrange("p (g w) -> p g w", w=32), ALU.add))
                    last_step()
                    nc.vector.tensor_tensor(state_bd[:, :, :].rearrange("p g (q w) -> p g q w", w=32),
                                            state[:, :, :].unsqueeze(2).to_broadcast([P, GB, P // 32, 32]),
                                            head_ones[:, :].rearrange("p (q w) -> p q w", w=32).unsqueeze(1).to_broadcast([P, GB, P // 32, 32]),
                                            ALU.mult).then_inc(state_ready, 1)
                assert count[0] == STEP_O, (count[0], STEP_O)
                for j, (t, w, r0, nr) in enumerate(QK):
                    ps = use(U_QK + j)
                    o = qk_u[:, j % 2, 0:nr * w].rearrange("p (r w) -> p r w", w=w)
                    nc.vector.tensor_tensor(o, ps[:, 0:nr * w].rearrange("p (r w) -> p r w", w=w),
                                            runs(U[:, :])[:, r0:r0 + nr, 0:w], ALU.mult).then_inc(att_read_v, 1)
                    dve.wait_ge(att_read_v, s * AV + reads(ATT_USES, "V", U_QK + j))
                    last = nc.vector.tensor_reduce(runs(O_in[:, :])[:, r0:r0 + nr, t], o, AX.X, ALU.add)
                step(last)
                last_step()
                dve.wait_ge(q_saved, s * CH + CH)
                nc.vector.tensor_tensor(O[:, :], O[:, :], O_in[:, :], ALU.add).then_inc(o_ready, 1)
                dve.wait_ge(y_added, s * 1 + 1)
                for m in range(KT_IN):
                    ps = use(U_OUT + m)
                    nc.vector.scalar_tensor_tensor(xs[:, m, :], ps[:, :], p("b_out", m), xs[:, m, :],
                                                   ALU.add, ALU.add).then_inc(att_read_v, 1)

            with dve.Fori(0, SLABS) as s:
                ffn(s * 2, s)
                attention(s)
                ffn(s * 2 + 1, s)

        @block.tensor
        def _(pe):
            def freed(uses, banks, j, read_v, read_s, v0, s0):
                k = j - banks
                who = uses[k]
                if who == "V":
                    pe.wait_ge(read_v, v0 + (reads(uses, "V", k) if k >= 0 else reads(uses, "V", k % len(uses)) - uses.count("V")))
                else:
                    pe.wait_ge(read_s, s0 + (reads(uses, "S", k) if k >= 0 else reads(uses, "S", k % len(uses)) - uses.count("S")))

            def ffn(n, s):
                xs = slab(s)

                def use(j):
                    if j >= FFN_BANKS:
                        freed(FFN_USES, FFN_BANKS, j, ffn_read_v, ffn_read_s, n * FV, n * FS)
                    return ffn_bank[j % FFN_BANKS]

                ps = use(0)
                for k in range(KT_IN):
                    mm = nc.tensor.matmul(ps[:, :], average[:, :], xs[:, k, :], start=k == 0, stop=k == KT_IN - 1)
                mm.then_inc(ffn_filled, 1)
                ps = use(1)
                pe.wait_ge(ffn_squared, n * 1 + 1)
                for k in range(KT_IN):
                    mm = nc.tensor.matmul(ps[:, :], average[:, :], xsq[:, k, :], start=k == 0, stop=k == KT_IN - 1)
                mm.then_inc(ffn_filled, 1)
                pe.wait_ge(w12_loaded, 32)
                pe.wait_ge(ffn_lo, n * 1 + 1)
                for m in range(KT_FF):
                    for half, w in enumerate((w1_sb, w2_sb)):
                        ps = use(2 + 2 * m + half)
                        for k in range(KT_IN):
                            for part, v in enumerate((xn_hi, xn_lo)):
                                mm = nc.tensor.matmul(ps[:, :], w[:, k, m * P:(m + 1) * P], v[:, k, :],
                                                      start=k == 0 and part == 0, stop=k == KT_IN - 1 and part == 1)
                        mm.then_inc(ffn_filled, 1)
                for layer, (w, loaded, tiles) in enumerate(((h1_sb, h1_loaded, KT_FF), (h2_sb, h2_loaded, KT_FF), (w3_sb, w3_loaded, KT_IN))):
                    pe.wait_ge(loaded, 16)
                    src = layer % 2
                    for m0 in range(0, tiles, 2):
                        j = 2 + (2 + layer) * KT_FF + m0
                        ps = [use(j), use(j + 1)]
                        for k in range(KT_FF):
                            if m0 == 0:
                                pe.wait_ge(hid_lo_ready, n * UNITS + layer * KT_FF + k + 1)
                            for m in range(2):
                                for part, v in enumerate((hid_hi[src], hid_lo[src])):
                                    mm = nc.tensor.matmul(ps[m][:, :], w[:, k, (m0 + m) * P:(m0 + m + 1) * P], v[:, k, :],
                                                          start=k == 0 and part == 0, stop=k == KT_FF - 1 and part == 1)
                                if k == KT_FF - 1:
                                    mm.then_inc(ffn_filled, 1)

            def attention(s):
                xs = slab(s)

                def use(j):
                    if j >= ATT_BANKS:
                        freed(ATT_USES, ATT_BANKS, j, att_read_v, att_read_s, s * AV, s * AS)
                    return att_bank[j % ATT_BANKS]

                def sums(j, ones, moving, count):
                    ps = use(j)
                    for k in range(count):
                        mm = nc.tensor.matmul(ps[:, 0:moving[k].shape[-1]], ones[:, :], moving[k], start=k == 0, stop=k == count - 1)
                    mm.then_inc(att_filled, 1)

                sums(0, average, [xs[:, k, :] for k in range(KT_IN)], KT_IN)
                pe.wait_ge(att_squared, s * 1 + 1)
                sums(1, average, [xsq[:, k, :] for k in range(KT_IN)], KT_IN)
                pe.wait_ge(att_w_loaded, 32)
                pe.wait_ge(att_normed, s * KT_IN + KT_IN)
                for j in range(4 * KT_IN):
                    ps = use(U_PROJ + j)
                    for k in range(KT_IN):
                        mm = nc.tensor.matmul(ps[:, :], wqkvb_sb[:, k, j * P:(j + 1) * P], xsq[:, k, :], start=k == 0, stop=k == KT_IN - 1)
                    mm.then_inc(att_filled, 1)
                pe.wait_ge(att_read_s, s * AS + 2 * KT_IN)
                for g in range(KT_IN):
                    sums(U_NORM + g, head_ones, [k_sq[:, g * N:(g + 1) * N]], 1)

                def dots(first, widths, ones):
                    for q, w in enumerate(widths, first):
                        pe.wait_ge(pairs_ready, s * (HALVES * len(KK) + len(QK)) + q + 1)
                        sums(U_KK + q, ones, [pairs[:, q % 3, 0:w]], 1)

                for c in range(CH):
                    if c % HCH == 0:
                        dots(c // HCH * len(KK), [HRUNS * w for _, w in KK], head_minus)
                    pe.wait_ge(state_ready, s * CH + c + 1)
                    for g in range(GB):
                        cols = KQ[:, :, :].rearrange("p w (i n) -> p w i n", n=32)[:, :, (g // 2) * CH + c, (g % 2) * C:(g % 2 + 1) * C]
                        mm = nc.tensor.matmul(retr_ps[:, g * 2 * C:(g + 1) * 2 * C], state_bd[:, g, :], cols, start=True, stop=True)
                    mm.then_inc(retr_ready, 1)
                    pe.wait_ge(kz_ready, s * 2 * CH + 2 * c + 2)
                    pe.wait_ge(u_turned, s * CH + c + 1)
                    pe.wait_ge(q_saved, s * CH + c + 1)
                    for g in range(GB):
                        mm = nc.tensor.matmul(dstate_ps[:, g * 32:(g + 1) * 32], Kz[:, c % 2, g, :], UTr[:, g // 2, :], start=True, stop=True)
                    mm.then_inc(dstate_ready, 1)
                dots(HALVES * len(KK), [nr * w for _, w, _, nr in QK], head_ones)
                pe.wait_ge(o_ready, s * 1 + 1)
                for m in range(KT_IN):
                    ps = use(U_OUT + m)
                    for k in range(KT_IN):
                        mm = nc.tensor.matmul(ps[:, :], wout_sb[:, k, m * P:(m + 1) * P], O[:, k * N:(k + 1) * N], start=k == 0, stop=k == KT_IN - 1)
                    mm.then_inc(att_filled, 1)

            pe.wait_ge(masks_ready, 3)
            with pe.Fori(0, SLABS) as s:
                pe.wait_ge(x_loaded, s * 16 + 16)
                ffn(s * 2, s)
                pe.wait_ge(ffn_read_v, (s * 2 + 1) * FV)
                attention(s)
                pe.wait_ge(att_read_v, (s + 1) * AV)
                ffn(s * 2 + 1, s)


def kernel(**inputs):
    import numpy as np
    import concourse.bacc as bacc
    from concourse.bass_utils import run_bass_kernel_spmd

    def of(name):
        return np.asarray(inputs["L0_" + name])

    def rows(a):
        return np.ascontiguousarray(a.reshape(-1, P, a.shape[-1]).transpose(1, 0, 2))

    x = of("attn_x").reshape(2, 2, SLABS, CH, C, KT_IN, P)
    x = np.ascontiguousarray(x.transpose(6, 2, 5, 0, 3, 1, 4)).reshape(P, SLABS, KT_IN, N)
    vectors = {"w1_s": "ffn_w1_s", "w2_s": "ffn_w2_s", "h1_s": "ffn_h1_s", "h2_s": "ffn_h2_s", "w3_s": "ffn_w3_s",
               "ln_g": "attn_ln_g", "ln_b": "attn_ln_b", "b_qkvb": "attn_b_qkvb", "b_out": "attn_b_out"}
    arrays = {
        "x": x,
        "w1": rows(of("ffn_w1_w").T), "w2": rows(of("ffn_w2_w").T),
        "h1": rows(of("ffn_h1_w").T), "h2": rows(of("ffn_h2_w").T), "w3": rows(of("ffn_w3_w").T),
        "wqkvb": rows(of("attn_w_qkvb")), "wout": rows(of("attn_w_out")),
        "par": np.ascontiguousarray(np.concatenate([of(vectors[n]).reshape(-1, P) for n in PAR]).T),
    }
    nc = bacc.Bacc("TRN2", target_bir_lowering=False, num_devices=1, dynamic_dma_scratch_size=4096)
    args = [nc.dram_tensor(f"in_{n}", list(a.shape), F32, kind="ExternalInput").ap() for n, a in arrays.items()]
    out = nc.dram_tensor("out", list(x.shape), F32, kind="ExternalOutput").ap()
    build(nc, *args, out)
    r = run_bass_kernel_spmd(nc, [{f"in_{n}": a for n, a in arrays.items()}], core_ids=[0])
    y = np.asarray(r.results[0]["out"]).reshape(P, SLABS, KT_IN, 2, CH, 2, C)
    return np.ascontiguousarray(y.transpose(3, 5, 1, 4, 6, 2, 0)).reshape(B, T, HID)
```

```python
from contextlib import ExitStack

import concourse.bass as bass
from concourse import mybir

F32 = mybir.dt.float32
F16 = mybir.dt.float16
ALU = mybir.AluOpType
ACT = mybir.ActivationFunctionType
AX = mybir.AxisListType

P = 128
B, T, HID = 4, 1024, 256
NH, D = 16, 16
FF = 1024
LN_EPS = 1e-5
NORM_EPS = 1e-6

KT_IN = HID // P
KT_FF = FF // P
SLAB_T = 128
SLABS = T // SLAB_T
N = B * SLAB_T
C = 16
CH = SLAB_T // C
HP = P // D
QUADS = P // 32
GB = KT_IN * B
GP = GB // 2
ITEMS = GP * CH
RUNS = 2 * ITEMS
COLS = KT_IN * N
HALVES = 2
HCH = CH // HALVES
HRUNS = RUNS // HALVES
RING = 4

PAR = {}
for _name, _n in (("w1_s", KT_FF), ("w2_s", KT_FF), ("h1_s", KT_FF), ("h2_s", KT_FF), ("w3_s", KT_IN),
                  ("ln_g", KT_IN), ("ln_b", KT_IN), ("b_qkvb", 4 * KT_IN), ("b_out", KT_IN)):
    PAR[_name] = (sum(n for _, n in PAR.values()), _n)
NPAR = sum(n for _, n in PAR.values())

W_AT = {}
for _name, _n in (("w1", KT_IN * FF), ("w2", KT_IN * FF), ("h1", KT_FF * FF), ("h2", KT_FF * FF), ("w3", KT_FF * HID)):
    W_AT[_name] = (sum(n for _, n in W_AT.values()), _n)
W_COLS = sum(n for _, n in W_AT.values())
W_PIECE = 2048
W_PIECES = W_COLS // W_PIECE
W_STAGES = 3
W_DONE = {name: -(-(at + n) // W_PIECE) for name, (at, n) in W_AT.items()}

KK = [(t, t) for t in range(1, C)]
QK = [(t, t + 1) for t in range(C)]
KK_AT = [HRUNS * t * (t - 1) // 2 for t in range(C + 1)]
DOTS = HALVES * (len(KK) + len(QK))
DOT_KK = [h * len(KK) for h in range(HALVES)]
DOT_QK = [HALVES * len(KK) + h * len(QK) for h in range(HALVES)]
PAIR_BUFFERS = 3

L1, L2, L3, LO = 0, 2 * KT_FF, 2 * KT_FF + 4 * KT_FF, 2 * KT_FF + 8 * KT_FF
SLOTS = LO + KT_FF
FFN_BANKS = 4
FFN_S, FFN_V = 4 * KT_FF, KT_IN
FFN_U = FFN_S + FFN_V
UNITS = 3 * KT_FF

ATT_BANKS = 2
PROJ = [2, 3, 0, 1, 6, 7, 4, 5]
ATT_USES = "VV" + "SSSS" + "VV" + "SSSS" + "V" * DOTS + "VV"
U_PROJ = [2, 3, 4, 5, 8, 9, 10, 11]
U_NORM = 6
U_DOTS = 12
U_OUT = U_DOTS + DOTS
ATT_U = len(ATT_USES)
AV, AS = ATT_USES.count("V"), ATT_USES.count("S")

STEP_ROOTS = 2
STEP_NORMED = STEP_ROOTS + 1
STEP_KNORM = STEP_NORMED + 1
CHUNK_STEPS = 2 + 2 * (C - 1) + 1
ATT_STEPS = STEP_KNORM + CH * CHUNK_STEPS + 1

E_MEAN, E_VAR = 2, 6
E_PROJ = [12, 13, 14, 15, 17, 18, 19, 20]
E_NORM = 16
E_KK0 = 26
E_RETR = [34 + 14 * c for c in range(CH)]
E_STATE = [e + 10 for e in E_RETR]
E_QK1 = E_STATE[-1] + 2
E_OUT = E_QK1 + 22
E_LN = ((36, 52), (106, 122))
LN_CHUNKS = ((0, 1, 2), (5, 6, 7))


def reads(who, j):
    return ATT_USES[:j + 1].count(who)


def dots_beside(c):
    if c < 3:
        return range(DOT_KK[1] + 5 * c, DOT_KK[1] + 5 * c + 5)
    if c >= HCH:
        return range(DOT_QK[0] + 4 * (c - HCH), DOT_QK[0] + 4 * (c - HCH) + 4)
    return range(0)


def dot(q):
    if q < DOT_QK[0]:
        h, j = divmod(q, len(KK))
        return (False, h) + KK[j]
    h, j = divmod(q - DOT_QK[0], len(QK))
    return (True, h) + QK[j]


def events(slot, calls):
    return (slot,) if calls == 2 else (2 * slot, 2 * slot + 1)


def build(nc, x, w, wqkvb, wout, par, out):
    with ExitStack() as ctx:
        def sb(name, shape, dt=F32):
            return ctx.enter_context(nc.sbuf_tensor(name, shape, dt))

        def bank(name):
            return ctx.enter_context(nc.psum_tensor(name, [P, 512], F32))

        def sem(name):
            return ctx.enter_context(nc.semaphore(name))

        w_sb = sb("w_sb", [P, W_COLS], F16)
        wqkvb_sb = sb("wqkvb_sb", [P, KT_IN, 4 * HID])
        wout_sb = sb("wout_sb", [P, KT_IN, HID])
        par_sb = sb("par_sb", [P, NPAR])
        w3_half = sb("w3_half", [P, KT_IN])
        ln_gain = sb("ln_gain", [P, KT_IN])
        average = sb("average", [P, P])
        head_ones = sb("head_ones", [P, P])
        head_minus = sb("head_minus", [P, P])
        quad_ones = sb("quad_ones", [P, QUADS])
        side_ones = sb("side_ones", [P, 2])
        X = sb("X", [P, RING, KT_IN, N])
        xc = sb("xc", [P, KT_IN, N])
        xn = sb("xn", [P, KT_IN, N])
        rstd = sb("rstd", [P, N])
        xn_hi = sb("xn_hi", [P, KT_IN, N], F16)
        xn_lo = sb("xn_lo", [P, KT_IN, N], F16)
        gate = sb("gate", [P, 2, N])
        hid = sb("hid", [P, 3, N])
        hid_hi = [sb(f"hid_hi{i}", [P, KT_FF, N], F16) for i in range(2)]
        hid_lo = [sb(f"hid_lo{i}", [P, KT_FF, N], F16) for i in range(2)]
        KQ = sb("KQ", [P, 2, COLS])
        V = sb("V", [P, COLS])
        beta = sb("beta", [P, COLS])
        U = sb("U", [P, COLS])
        O = sb("O", [P, COLS])
        k_sq = O
        O_in = sb("O_in", [P, COLS])
        k_raw = O_in
        NK = sb("NK", [P, HALVES, KK_AT[C]])
        stage = NK[:, :, :].rearrange("p h n -> p (h n)")
        pairs = sb("pairs", [P, PAIR_BUFFERS, N])
        qk_u = sb("qk_u", [P, 2, N])
        roots = qk_u
        KTr = sb("KTr", [P, ITEMS, 32])
        Kz = sb("Kz", [P, 2, GP, P])
        UTr = sb("UTr", [P, GP, 32])
        Uz = sb("Uz", [P, GP, 2, 32])
        terms = sb("terms", [P, C, GB, C])
        before = terms[:, :, :, :].rearrange("p t g w -> p (t g w)")
        axc = before[:, 0:COLS].rearrange("p (k n) -> p k n", k=KT_IN)
        an = before[:, COLS:2 * COLS].rearrange("p (k n) -> p k n", k=KT_IN)
        resid = sb("resid", [P, GB, C])
        state = sb("state", [P, GB, 32])
        state_bd = sb("state_bd", [P, GB, P])

        ffn_bank = [bank(f"ffn_bank{i}") for i in range(FFN_BANKS)]
        ln_bank = bank("ln_bank")
        att_bank = [bank(f"att_bank{i}") for i in range(ATT_BANKS)]
        state_bank = bank("state_bank")
        retr_ps = state_bank[:, 0:GB * 2 * C]
        dstate_ps = state_bank[:, 256:512]

        x_loaded, par_loaded, att_w_loaded, w_staged, stored = (sem(n) for n in (
            "x_loaded", "par_loaded", "att_w_loaded", "w_staged", "stored"))
        masks_step, masks_ready, side_ready, consts_ready, state_zeroed, w_ready = (sem(n) for n in (
            "masks_step", "masks_ready", "side_ready", "consts_ready", "state_zeroed", "w_ready"))
        ln_filled, ln_read, ln_squared, ln_inverted, ln_rooted, ln_normed, ln_hi, ln_lo = (sem(n) for n in (
            "ln_filled", "ln_read", "ln_squared", "ln_inverted", "ln_rooted", "ln_normed", "ln_hi", "ln_lo"))
        ffn_filled, ffn_read, ffn_added = sem("ffn_filled"), sem("ffn_read"), sem("ffn_added")
        hid_mixed, hid_hi_ready, hid_lo_ready = sem("hid_mixed"), sem("hid_hi_ready"), sem("hid_lo_ready")
        att_filled, att_read_v, att_read_s = sem("att_filled"), sem("att_read_v"), sem("att_read_s")
        att_squared, att_rooted, att_normed, k_rooted = (sem(n) for n in (
            "att_squared", "att_rooted", "att_normed", "k_rooted"))
        y_scaled, y_added, k_ready, k_turned, pairs_ready, kz_ready = (sem(n) for n in (
            "y_scaled", "y_added", "k_ready", "k_turned", "pairs_ready", "kz_ready"))
        retr_ready, resid_ready, q_saved, u_turned, u_ready, dstate_ready, state_ready = (sem(n) for n in (
            "retr_ready", "resid_ready", "q_saved", "u_turned", "u_ready", "dstate_ready", "state_ready"))
        att_step, o_ready = sem("att_step"), sem("o_ready")

        def p(name, j):
            a = PAR[name][0] + j
            return par_sb[:, a:a + 1]

        def weight(name, k, m):
            at, n = W_AT[name]
            width = HID if name == "w3" else FF
            a = at + k * width + m * P
            return w_sb[:, a:a + P]

        def slab(s):
            return X[:, bass.ds(s % RING, 1), :, :].rearrange("p s k n -> p (s k) n")

        def both(ap):
            return ap.unsqueeze(1).to_broadcast([P, KT_IN, N])

        def half(ap, h):
            return ap.rearrange("p (g h r t) -> p g h r t", h=HALVES, r=2 * HCH, t=C)[:, :, h, :, :]

        def at_chunk(ap, c):
            return ap.rearrange("p (g c b t) -> p g c b t", c=CH, b=2, t=C)[:, :, c, :, :]

        def packed(ap, n):
            return ap.rearrange("p (g r w) -> p g r w", g=GP, w=n)

        def nk_row(t, c):
            row = NK[:, c // HCH, KK_AT[t]:KK_AT[t + 1]]
            return row.rearrange("p (g c b t) -> p g c b t", c=HCH, b=2, t=t)[:, :, c % HCH, :, :]

        def four(ap):
            return ap.rearrange("p (g b) t -> p g b t", b=2)

        def ffn_ps(off, j):
            return ffn_bank[(off + j) % FFN_BANKS][:, :]

        def pair_buffer(q):
            w = dot(q)[3]
            return pairs[:, q % PAIR_BUFFERS, 0:HRUNS * w], w

        block = ctx.enter_context(nc.Block())

        FIRST, SECOND = (0, 0, 0), (1, 2, 1)
        LAST2, LAST = (2 * SLABS - 2, 0, SLABS - 2), (2 * SLABS - 1, 2, SLABS - 1)

        def calls_of(s):
            return (s * 2, 0, s + 1), (s * 2 + 1, 2, s - 1)

        def run(eng, alone, iteration):
            alone(FIRST, True)
            iteration(0, SECOND, None, (2, 0, 2))
            with eng.Fori(1, SLABS - 2) as s:
                a, b = calls_of(s)
                iteration(s, a, b, (s * 2 + 2, 0, s + 2))
            a, b = calls_of(SLABS - 2)
            iteration(SLABS - 2, a, b, None)
            iteration(SLABS - 1, None, LAST2, None)
            alone(LAST, False)

        @block.sync
        def _(sp):
            def load(s, slot):
                sp.dma_start(X[:, bass.ds(slot, 1), :, :], x[:, bass.ds(s, 1), :, :]).then_inc(x_loaded, 16)

            def store(s, slot):
                sp.dma_start(out[:, bass.ds(s, 1), :, :], X[:, bass.ds(slot, 1), :, :]).then_inc(stored, 16)

            def stage_piece(i):
                if i >= W_STAGES:
                    sp.wait_ge(w_ready, i - W_STAGES + 1)
                a = i % W_STAGES * W_PIECE
                sp.dma_start(stage[:, a:a + W_PIECE], w[:, i * W_PIECE:(i + 1) * W_PIECE]).then_inc(w_staged, 16)
                sp.wait_ge(w_staged, 16 * (i + 1))

            sp.dma_start(par_sb[:, :], par).then_inc(par_loaded, 16)
            load(0, 0)
            sp.wait_ge(x_loaded, 16)
            for i in range(W_PIECES):
                stage_piece(i)
                if i == 2:
                    load(1, 1)
            sp.dma_start(wqkvb_sb[:, :, :], wqkvb).then_inc(att_w_loaded, 16)
            sp.dma_start(wout_sb[:, :, :], wout).then_inc(att_w_loaded, 16)
            for s in range(2, RING):
                sp.wait_ge(x_loaded, 16 * s)
                load(s, s)
            with sp.Fori(0, SLABS - RING) as s:
                sp.wait_ge(ffn_added, (s * 2 + 4) * FFN_V)
                store(s, s % RING)
                sp.wait_ge(stored, (s + 1) * 16)
                sp.wait_ge(x_loaded, s * 16 + 16 * RING)
                load(s + RING, s % RING)
            for s in range(SLABS - RING, SLABS):
                sp.wait_ge(ffn_added, ((2 * s + 3 if s < SLABS - 2 else SLABS + s) + 1) * FFN_V)
                store(s, s % RING)
            sp.wait_ge(stored, 16 * SLABS)

        @block.gpsimd
        def _(pool):
            pool.memset(average[:, :], 1.0 / HID).then_inc(masks_ready, 1)
            for n, (m, v) in enumerate(((head_ones, 1.0), (head_minus, -1.0))):
                pool.memset(m[:, :], v).then_inc(masks_step, 1)
                pool.wait_ge(masks_step, 2 * n + 1)
                view = m[:, :].rearrange("p (h i) -> p h i", i=D)
                pool.affine_select(out=view, in_=view, compare_op=ALU.is_ge, fill=0.0, base=0,
                                   pattern=[[-D, HP], [0, D]], channel_multiplier=1).then_inc(masks_step, 1)
                pool.wait_ge(masks_step, 2 * n + 2)
                pool.affine_select(out=view, in_=view, compare_op=ALU.is_ge, fill=0.0, base=D - 1,
                                   pattern=[[D, HP], [0, D]], channel_multiplier=-1).then_inc(masks_ready, 1)
            pool.memset(state[:, :, :], 0.0).then_inc(state_zeroed, 1)
            pool.memset(state_bd[:, :, :], 0.0).then_inc(state_ready, 1)
            pool.wait_ge(side_ready, 2)

            def ln_low(call):
                n, _, _ = call
                pool.wait_ge(ln_hi, n * 1 + 1)
                pool.tensor_tensor(xn_lo[:, :, :], xn[:, :, :], xn_hi[:, :, :], ALU.subtract).then_inc(ln_lo, 1)

            def low(n, u):
                layer, m = divmod(u, KT_FF)
                pool.wait_ge(hid_hi_ready, n * UNITS + (u + 1))
                pool.tensor_tensor(hid_lo[layer % 2][:, m, :], hid[:, u % 3, :], hid_hi[layer % 2][:, m, :],
                                   ALU.subtract).then_inc(hid_lo_ready, 1)

            def ffn(call, k):
                n, _, _ = call
                if k < L2 and k % 2:
                    m = k // 2
                    pool.wait_ge(ffn_read, n * FFN_S + (2 * m + 2))
                    pool.tensor_tensor(hid[:, m % 3, :], hid[:, m % 3, :], gate[:, m % 2, :], ALU.mult).then_inc(hid_mixed, 1)
                    if m >= 1:
                        low(n, m - 1)
                elif k == L2:
                    low(n, KT_FF - 1)
                elif L2 <= k < LO and k % 8 == 7:
                    u = KT_FF + (k - L2) // 8 * 2
                    low(n, u)
                    low(n, u + 1)

            def add_y(s):
                pool.wait_ge(att_step, s * ATT_STEPS + STEP_NORMED)
                pool.tensor_tensor(axc, axc, both(roots[:, 0, :]), ALU.mult).then_inc(y_scaled, 1)
                pool.wait_ge(y_scaled, s * 1 + 1)
                pool.tensor_tensor(slab(s), slab(s), axc, ALU.add).then_inc(y_added, 1)

            def make_pairs(s, q):
                of_q, h, t, w = dot(q)
                if q >= PAIR_BUFFERS:
                    pool.wait_ge(att_filled, s * ATT_U + (U_DOTS + q - PAIR_BUFFERS + 1))
                buf, _ = pair_buffer(q)
                later = half(KQ[:, 1 if of_q else 0, :], h)[:, :, :, t:t + 1].to_broadcast([P, GP, 2 * HCH, w])
                pool.tensor_tensor(packed(buf, w), later, half(KQ[:, 0, :], h)[:, :, :, 0:w], ALU.mult).then_inc(pairs_ready, 1)

            def make_kz(s, c):
                if c >= 2:
                    pool.wait_ge(dstate_ready, s * CH + (c - 1))
                keys = KTr[:, :, :].rearrange("p (g c) w -> p g c w", c=CH)[:, :, c:c + 1, :]
                pool.tensor_tensor(Kz[:, c % 2, :, :].rearrange("p g (q w) -> p g q w", w=32),
                                   keys.to_broadcast([P, GP, QUADS, 32]),
                                   quad_ones[:, :].unsqueeze(1).unsqueeze(3).to_broadcast([P, GP, QUADS, 32]),
                                   ALU.mult).then_inc(kz_ready, 1)

            def attention(s, e):
                if e == E_VAR + 4:
                    add_y(s)
                if e == E_KK0 - 2:
                    pool.wait_ge(k_ready, s * KT_IN + KT_IN)
                if E_KK0 - 2 <= e < E_KK0 + 6:
                    for q in range(2 * (e - E_KK0 + 2), min(2 * (e - E_KK0 + 2) + 2, len(KK))):
                        make_pairs(s, q)
                for c in range(CH):
                    if e == E_RETR[c]:
                        if c == 0:
                            pool.wait_ge(k_turned, s * 1 + 1)
                        make_kz(s, c)
                    beside = dots_beside(c)
                    if 0 <= e - E_RETR[c] < len(beside):
                        make_pairs(s, beside[e - E_RETR[c]])
                if 0 <= e - E_STATE[-1] < len(QK):
                    make_pairs(s, DOT_QK[1] + e - E_STATE[-1])

            def ln_next(e, call, which):
                if call and e == (80, 160)[which]:
                    ln_low(call)

            def alone(call, first):
                ln_low(call)
                for k in range(SLOTS):
                    ffn(call, k)
                    if first and k == 80:
                        ln_low(SECOND)

            def iteration(s, a, b, nxt):
                calls = [c for c in (a, b) if c]
                if not a:
                    ln_low(b)
                for slot in range(SLOTS * len(calls)):
                    for e in events(slot, len(calls)):
                        attention(s, e)
                        if a:
                            ln_next(e, b, 0)
                        ln_next(e, nxt, 1)
                    ffn(calls[slot // SLOTS], slot % SLOTS)

            run(pool, alone, iteration)

        @block.scalar
        def _(act):
            act.wait_ge(par_loaded, 16)
            act.mul(w3_half[:, :], par_sb[:, PAR["w3_s"][0]:PAR["w3_s"][0] + KT_IN], 0.5).then_inc(consts_ready, 1)
            act.mul(ln_gain[:, :], par_sb[:, PAR["ln_g"][0]:PAR["ln_g"][0] + KT_IN],
                    (1.0 + LN_EPS) ** -0.5).then_inc(consts_ready, 1)
            act.wait_ge(consts_ready, 2)

            def ln_square(call):
                n, _, _ = call
                act.wait_ge(ln_read, n * 2 + 1)
                act.activation(xn[:, :, :], xc[:, :, :], ACT.Square).then_inc(ln_squared, 1)

            def ln_root(call):
                n, _, _ = call
                act.wait_ge(ln_inverted, n * 1 + 1)
                act.activation(rstd[:, :], rstd[:, :], ACT.Sqrt).then_inc(ln_rooted, 1)

            def ln_high(call):
                n, _, _ = call
                act.wait_ge(ln_normed, n * 1 + 1)
                act.copy(xn_hi[:, :, :], xn[:, :, :]).then_inc(ln_hi, 1)

            def high(n, u):
                layer, m = divmod(u, KT_FF)
                if u < KT_FF:
                    act.wait_ge(hid_mixed, n * KT_FF + (u + 1))
                act.copy(hid_hi[layer % 2][:, m, :], hid[:, u % 3, :]).then_inc(hid_hi_ready, 1)

            def ffn(call, k):
                n, off, _ = call
                if k < L2:
                    m = k // 2
                    act.wait_ge(ffn_filled, n * FFN_U + (k + 1))
                    if k % 2 == 0:
                        if m >= 2:
                            act.wait_ge(hid_mixed, n * KT_FF + (m - 1))
                        act.activation(gate[:, m % 2, :], ffn_ps(off, k), ACT.Silu, scale=p("w1_s", m)).then_inc(ffn_read, 1)
                    else:
                        if m >= 3:
                            act.wait_ge(hid_lo_ready, n * UNITS + (m - 2))
                        act.activation(hid[:, m % 3, :], ffn_ps(off, k), ACT.Copy, scale=p("w2_s", m)).then_inc(ffn_read, 1)
                        if m >= 1:
                            high(n, m - 1)
                elif k == L2:
                    high(n, KT_FF - 1)
                elif L2 <= k < LO and k % 8 == 7:
                    u = KT_FF + (k - L2) // 8 * 2
                    for i in range(2):
                        j = KT_FF + u + i
                        layer, m = divmod(u + i, KT_FF)
                        act.wait_ge(ffn_filled, n * FFN_U + (j + 1))
                        act.wait_ge(hid_lo_ready, n * UNITS + (u + i - 2))
                        act.activation(hid[:, (u + i) % 3, :], ffn_ps(off, j), ACT.Gelu,
                                       scale=p(("h1_s", "h2_s")[layer - 1], m)).then_inc(ffn_read, 1)
                    for i in range(2):
                        act.wait_ge(ffn_read, n * FFN_S + (KT_FF + u + i + 1))
                        high(n, u + i)

            def project(s, i):
                j, use = PROJ[i], U_PROJ[i]
                which, g = divmod(j, KT_IN)
                cols = slice(g * N, (g + 1) * N)
                ps = att_bank[use % ATT_BANKS][:, :]
                dest = (KQ[:, 1, cols], k_raw[:, cols], V[:, cols], beta[:, cols])[which]
                act.wait_ge(att_filled, s * ATT_U + (use + 1))
                if which == 1:
                    act.activation(k_sq[:, cols], ps, ACT.Square, bias=p("b_qkvb", j))
                act.activation(dest, ps, ACT.Sigmoid if which == 3 else ACT.Identity, bias=p("b_qkvb", j)).then_inc(att_read_s, 1)

            def attention(s, e):
                if e == E_MEAN + 2:
                    act.wait_ge(att_read_v, s * AV + 1)
                    act.activation(an, axc, ACT.Square).then_inc(att_squared, 1)
                if e == E_VAR + 2:
                    act.wait_ge(att_step, s * ATT_STEPS + STEP_ROOTS)
                    act.activation(roots[:, :, :], roots[:, :, :], ACT.Sqrt).then_inc(att_rooted, 1)
                if e == E_VAR + 5:
                    act.wait_ge(att_step, s * ATT_STEPS + STEP_NORMED)
                    for k in range(KT_IN):
                        act.activation(an[:, k, :], an[:, k, :], ACT.Identity, scale=ln_gain[:, k:k + 1],
                                       bias=p("ln_b", k)).then_inc(att_normed, 1)
                for i in range(len(PROJ)):
                    if e == E_PROJ[i]:
                        project(s, i)
                if e == E_PROJ[-1] + 1:
                    act.wait_ge(att_step, s * ATT_STEPS + STEP_KNORM)
                    act.activation(k_sq[:, :], k_sq[:, :], ACT.Sqrt).then_inc(k_rooted, 1)
                for c in range(CH):
                    if e == E_RETR[c] + 2:
                        act.wait_ge(resid_ready, s * CH + (c + 1))
                        act.copy(at_chunk(O[:, :], c), four(retr_ps.rearrange("p (g w) -> p g w", w=2 * C)[:, :, C:2 * C])).then_inc(q_saved, 1)

            def ln_next(e, call, which):
                if call and e == E_LN[which][0] + 10:
                    ln_square(call)
                if call and e == E_LN[which][1] + 8:
                    ln_root(call)
                if call and e == E_LN[which][1] + 24:
                    ln_high(call)

            def alone(call, first):
                ln_square(call)
                ln_root(call)
                ln_high(call)
                for k in range(SLOTS):
                    ffn(call, k)
                    if first and k == 50:
                        ln_square(SECOND)
                    if first and k == 60:
                        ln_root(SECOND)
                    if first and k == 70:
                        ln_high(SECOND)

            def iteration(s, a, b, nxt):
                calls = [c for c in (a, b) if c]
                if not a:
                    ln_square(b)
                    ln_root(b)
                    ln_high(b)
                for slot in range(SLOTS * len(calls)):
                    for e in events(slot, len(calls)):
                        attention(s, e)
                        if a:
                            ln_next(e, b, 0)
                        ln_next(e, nxt, 1)
                    ffn(calls[slot // SLOTS], slot % SLOTS)

            run(act, alone, iteration)

        @block.vector
        def _(dve):
            dve.wait_ge(masks_ready, 3)
            of_head = head_ones[:, :].rearrange("p (q b w) -> p q b w", b=2, w=D)[:, :, :, 0]
            nc.vector.tensor_reduce(quad_ones[:, :], of_head, AX.X, ALU.add).then_inc(side_ready, 1)
            nc.vector.tensor_reduce(side_ones[:, :], of_head.rearrange("p q b -> p b q"), AX.X, ALU.add).then_inc(side_ready, 1)
            dve.wait_ge(consts_ready, 2)
            dve.wait_ge(state_zeroed, 1)
            dve.wait_ge(side_ready, 2)

            def convert(i):
                a = i % W_STAGES * W_PIECE
                dve.wait_ge(w_staged, 16 * (i + 1))
                nc.vector.tensor_copy(w_sb[:, i * W_PIECE:(i + 1) * W_PIECE], stage[:, a:a + W_PIECE]).then_inc(w_ready, 1)

            def ln_center(call):
                n, _, s = call
                dve.wait_ge(ln_filled, n * 2 + 1)
                nc.vector.tensor_tensor(xc[:, :, :], slab(s), both(ln_bank[:, :]), ALU.subtract).then_inc(ln_read, 1)

            def ln_invert(call):
                n, _, _ = call
                dve.wait_ge(ln_filled, n * 2 + 2)
                nc.vector.tensor_scalar(rstd[:, :], ln_bank[:, :], LN_EPS, None, ALU.add).then_inc(ln_read, 1)
                dve.wait_ge(ln_read, n * 2 + 2)
                nc.vector.reciprocal(rstd[:, :], rstd[:, :]).then_inc(ln_inverted, 1)

            def ln_norm(call):
                n, _, _ = call
                dve.wait_ge(ln_rooted, n * 1 + 1)
                nc.vector.tensor_tensor(xn[:, :, :], xc[:, :, :], both(rstd[:, :]), ALU.mult).then_inc(ln_normed, 1)

            def ffn_out(call):
                n, off, s = call
                xs = slab(s)
                for m in range(KT_IN):
                    j = FFN_S + m
                    dve.wait_ge(ffn_filled, n * FFN_U + (j + 1))
                    nc.vector.scalar_tensor_tensor(xs[:, m, :], ffn_ps(off, j), w3_half[:, m:m + 1],
                                                   xs[:, m, :], ALU.mult, ALU.add).then_inc(ffn_added, 1)

            def use(s, j):
                dve.wait_ge(att_filled, s * ATT_U + (j + 1))
                return att_bank[j % ATT_BANKS]

            def att_norm(s):
                nc.vector.tensor_tensor(axc, slab(s), both(use(s, 0)[:, :]), ALU.subtract).then_inc(att_read_v, 1)
                var = use(s, 1)
                nc.vector.tensor_scalar(roots[:, 0, :], var[:, :], LN_EPS, None, ALU.add).then_inc(att_step, 1)
                nc.vector.tensor_scalar(roots[:, 1, :], var[:, :], LN_EPS * LN_EPS / (1 + LN_EPS), None, ALU.add).then_inc(att_read_v, 1)
                dve.wait_ge(att_step, s * ATT_STEPS + 1)
                dve.wait_ge(att_read_v, s * AV + 2)
                nc.vector.reciprocal(roots[:, :, :], roots[:, :, :]).then_inc(att_step, 1)
                dve.wait_ge(att_rooted, s * 1 + 1)
                nc.vector.tensor_tensor(an, axc, both(roots[:, 1, :]), ALU.mult).then_inc(att_step, 1)

            def key_norm(s):
                for g in range(KT_IN):
                    ps = use(s, U_NORM + g)
                    nc.vector.tensor_scalar(k_sq[:, g * N:(g + 1) * N], ps[:, :], NORM_EPS * NORM_EPS, None, ALU.max).then_inc(att_read_v, 1)
                dve.wait_ge(att_read_v, s * AV + reads("V", U_NORM + 1))
                nc.vector.reciprocal(k_sq[:, :], k_sq[:, :]).then_inc(att_step, 1)
                dve.wait_ge(k_rooted, s * 1 + 1)
                for g in range(KT_IN):
                    cols = slice(g * N, (g + 1) * N)
                    nc.vector.tensor_tensor(KQ[:, 0, cols], k_raw[:, cols], k_sq[:, cols], ALU.mult).then_inc(k_ready, 1)
                dve.wait_ge(k_ready, s * KT_IN + KT_IN)
                nc.vector.transpose(KTr[:, :, :].rearrange("p i w -> p (i w)"), KQ[:, 0, :]).then_inc(k_turned, 1)

            def take_dots(s, q):
                of_q, h, t, w = dot(q)
                ps = packed(use(s, U_DOTS + q)[:, 0:HRUNS * w], w)
                if not of_q:
                    nc.vector.tensor_tensor(packed(NK[:, h, KK_AT[t]:KK_AT[t + 1]], w), ps,
                                            half(beta[:, :], h)[:, :, :, t:t + 1].to_broadcast([P, GP, 2 * HCH, w]),
                                            ALU.mult).then_inc(att_read_v, 1)
                    return
                buf = packed(qk_u[:, q % 2, 0:HRUNS * w], w)
                nc.vector.tensor_tensor(buf, ps, half(U[:, :], h)[:, :, :, 0:w], ALU.mult).then_inc(att_read_v, 1)
                dve.wait_ge(att_read_v, s * AV + reads("V", U_DOTS + q))
                done = nc.vector.tensor_reduce(half(O_in[:, :], h)[:, :, :, t], buf, AX.X, ALU.add)
                if q == DOTS - 1:
                    done.then_inc(att_step, 1)

            def chunk(s, c, beside):
                count = [STEP_KNORM + c * CHUNK_STEPS]

                def step(ins):
                    count[0] += 1
                    ins.then_inc(att_step, 1)

                def last_step():
                    dve.wait_ge(att_step, s * ATT_STEPS + count[0])

                if c % HCH == 0:
                    dve.wait_ge(att_read_v, s * AV + reads("V", U_DOTS + DOT_KK[c // HCH] + len(KK) - 1))
                if c == 0:
                    dve.wait_ge(att_read_s, s * AS + AS)
                    dve.wait_ge(y_added, s * 1 + 1)
                dots = list(dots_beside(c))
                dve.wait_ge(retr_ready, s * CH + (c + 1))
                retr = retr_ps.rearrange("p (g w) -> p g w", w=2 * C)[:, :, 0:C]
                nc.vector.tensor_tensor(four(resid[:, :, :]), at_chunk(V[:, :], c), four(retr), ALU.subtract).then_inc(resid_ready, 1)
                dve.wait_ge(resid_ready, s * CH + (c + 1))
                heads = terms[:, :, :, 0].rearrange("p t g -> p g t")
                step(nc.vector.tensor_tensor(four(heads), four(resid[:, :, :]), at_chunk(beta[:, :], c), ALU.mult))
                u = at_chunk(U[:, :], c)
                last_step()
                step(nc.vector.tensor_copy(u[:, :, :, 0], four(terms[:, 0, :, 0:1])[:, :, :, 0]))
                for t in range(1, C):
                    last_step()
                    step(nc.vector.tensor_tensor(four(terms[:, t, :, 1:t + 1]), nk_row(t, c), u[:, :, :, 0:t], ALU.mult))
                    last_step()
                    step(nc.vector.tensor_reduce(u[:, :, :, t], four(terms[:, t, :, 0:t + 1]), AX.X, ALU.add))
                    if dots and t >= C - 2 * len(dots) and t >= C // 2:
                        take_dots(s, dots.pop(0))
                last_step()
                nc.vector.transpose(UTr[:, :, :], u.rearrange("p g b t -> p g (b t)")).then_inc(u_turned, 1)
                dve.wait_ge(u_turned, s * CH + (c + 1))
                nc.vector.tensor_tensor(Uz[:, :, :, :], UTr[:, :, :].unsqueeze(2).to_broadcast([P, GP, 2, 32]),
                                        side_ones[:, :].unsqueeze(1).unsqueeze(3).to_broadcast([P, GP, 2, 32]),
                                        ALU.mult).then_inc(u_ready, 1)
                for q in dots:
                    take_dots(s, q)
                beside()
                dve.wait_ge(dstate_ready, s * CH + (c + 1))
                step(nc.vector.tensor_tensor(state[:, :, :], state[:, :, :], dstate_ps.rearrange("p (g w) -> p g w", w=32), ALU.add))
                last_step()
                nc.vector.tensor_tensor(state_bd[:, :, :].rearrange("p g (q w) -> p g q w", w=32),
                                        state[:, :, :].unsqueeze(2).to_broadcast([P, GB, QUADS, 32]),
                                        head_ones[:, :].rearrange("p (q w) -> p q w", w=32).unsqueeze(1).to_broadcast([P, GB, QUADS, 32]),
                                        ALU.mult).then_inc(state_ready, 1)

            def att_out(s):
                for q in range(DOT_QK[1], DOTS):
                    take_dots(s, q)
                dve.wait_ge(att_step, (s + 1) * ATT_STEPS)
                dve.wait_ge(q_saved, s * CH + CH)
                nc.vector.tensor_tensor(O[:, :], O[:, :], O_in[:, :], ALU.add).then_inc(o_ready, 1)
                xs = slab(s)
                for m in range(KT_IN):
                    ps = use(s, U_OUT + m)
                    nc.vector.scalar_tensor_tensor(xs[:, m, :], ps[:, :], p("b_out", m), xs[:, m, :],
                                                   ALU.add, ALU.add).then_inc(att_read_v, 1)

            def alone(call, first):
                ln_center(call)
                ln_invert(call)
                ln_norm(call)
                if first:
                    for i in range(W_PIECES):
                        convert(i)
                    ln_center(SECOND)
                    ln_invert(SECOND)
                    ln_norm(SECOND)
                ffn_out(call)

            def iteration(s, a, b, nxt):
                if not a:
                    ln_center(b)
                    ln_invert(b)
                    ln_norm(b)
                att_norm(s)
                key_norm(s)
                dve.wait_ge(att_read_s, s * AS + 6)
                for q in range(len(KK)):
                    take_dots(s, q)

                for c in range(CH):
                    def beside():
                        for call, chunks in ((b if a else None, LN_CHUNKS[0]), (nxt, LN_CHUNKS[1])):
                            if call and c in chunks:
                                (ln_center, ln_invert, ln_norm)[chunks.index(c)](call)
                    chunk(s, c, beside)
                    if c == HCH - 1 and a and b:
                        ffn_out(a)
                att_out(s)
                ffn_out(b or a)

            run(dve, alone, iteration)

        @block.tensor
        def _(pe):
            def ln_mean(call, first_ffn):
                n, _, s = call
                if first_ffn:
                    pe.wait_ge(x_loaded, s * 16 + 16)
                else:
                    pe.wait_ge(att_read_v, (s + 1) * AV)
                if n is not FIRST[0]:
                    pe.wait_ge(ln_read, n * 2)
                for k in range(KT_IN):
                    mm = nc.tensor.matmul(ln_bank[:, :], average[:, :], slab(s)[:, k, :], start=k == 0, stop=k == KT_IN - 1)
                mm.then_inc(ln_filled, 1)

            def ln_var(call):
                n, _, _ = call
                pe.wait_ge(ln_squared, n * 1 + 1)
                for k in range(KT_IN):
                    mm = nc.tensor.matmul(ln_bank[:, :], average[:, :], xn[:, k, :], start=k == 0, stop=k == KT_IN - 1)
                mm.then_inc(ln_filled, 1)

            def bank_free(call, j):
                n, _, _ = call
                i = j - FFN_BANKS
                if i >= 0:
                    pe.wait_ge(ffn_read, n * FFN_S + (i + 1))
                elif n is not FIRST[0]:
                    if i + FFN_V >= 0:
                        pe.wait_ge(ffn_added, n * FFN_V + (i + 1))
                    else:
                        pe.wait_ge(ffn_read, n * FFN_S + (i + FFN_V + 1))

            def ffn(call, k, starting=False):
                n, off, _ = call

                def loaded(name):
                    if starting:
                        pe.wait_ge(w_ready, W_DONE[name])

                if k < L2:
                    m, up = divmod(k, 2)
                    if k == 0:
                        loaded("w2")
                        pe.wait_ge(ln_lo, n * 1 + 1)
                    bank_free(call, k)
                    name = "w2" if up else "w1"
                    for kk in range(KT_IN):
                        for part, v in enumerate((xn_hi, xn_lo)):
                            mm = nc.tensor.matmul(ffn_ps(off, k), weight(name, kk, m), v[:, kk, :],
                                                  start=kk == 0 and part == 0, stop=kk == KT_IN - 1 and part == 1)
                    mm.then_inc(ffn_filled, 1)
                    return
                layer, name = (0, "h1") if k < L3 else (1, "h2") if k < LO else (2, "w3")
                pair, kk = divmod(k - (L2, L3, LO)[layer], KT_FF)
                if kk == 0:
                    if pair == 0:
                        loaded(name)
                    for i in range(2):
                        bank_free(call, 2 * KT_FF + layer * KT_FF + 2 * pair + i)
                if pair == 0:
                    pe.wait_ge(hid_lo_ready, n * UNITS + (layer * KT_FF + kk + 1))
                for i in range(2):
                    j = 2 * KT_FF + layer * KT_FF + 2 * pair + i
                    for part, v in enumerate((hid_hi[layer % 2], hid_lo[layer % 2])):
                        mm = nc.tensor.matmul(ffn_ps(off, j), weight(name, kk, 2 * pair + i), v[:, kk, :],
                                              start=kk == 0 and part == 0, stop=kk == KT_FF - 1 and part == 1)
                    if kk == KT_FF - 1:
                        mm.then_inc(ffn_filled, 1)

            def att_use(s, j):
                i = j - ATT_BANKS
                if i >= 0:
                    if ATT_USES[i] == "V":
                        pe.wait_ge(att_read_v, s * AV + reads("V", i))
                    else:
                        pe.wait_ge(att_read_s, s * AS + reads("S", i))
                elif s is not 0:
                    pe.wait_ge(att_read_v, s * AV + (i + 1))
                return att_bank[j % ATT_BANKS]

            def sums(s, j, ones, moving):
                ps = att_use(s, j)
                for k, m in enumerate(moving):
                    mm = nc.tensor.matmul(ps[:, 0:m.shape[-1]], ones[:, :], m, start=k == 0, stop=k == len(moving) - 1)
                mm.then_inc(att_filled, 1)

            def project(s, i):
                ps, j = att_use(s, U_PROJ[i]), PROJ[i]
                for k in range(KT_IN):
                    mm = nc.tensor.matmul(ps[:, :], wqkvb_sb[:, k, j * P:(j + 1) * P], an[:, k, :], start=k == 0, stop=k == KT_IN - 1)
                mm.then_inc(att_filled, 1)

            def dots(s, q):
                pe.wait_ge(pairs_ready, s * DOTS + (q + 1))
                sums(s, U_DOTS + q, head_ones if dot(q)[0] else head_minus, [pair_buffer(q)[0]])

            def retrieve(s, c):
                pe.wait_ge(state_ready, s * CH + (c + 1))
                for g in range(GB):
                    cols = KQ[:, :, :].rearrange("p w (i n) -> p w i n", n=32)[:, :, (g // 2) * CH + c, (g % 2) * C:(g % 2 + 1) * C]
                    mm = nc.tensor.matmul(retr_ps[:, g * 2 * C:(g + 1) * 2 * C], state_bd[:, g, :], cols, start=True, stop=True)
                mm.then_inc(retr_ready, 1)

            def update(s, c):
                pe.wait_ge(kz_ready, s * CH + (c + 1))
                pe.wait_ge(u_ready, s * CH + (c + 1))
                pe.wait_ge(q_saved, s * CH + (c + 1))
                for g in range(GP):
                    mm = nc.tensor.matmul(dstate_ps[:, g * 64:(g + 1) * 64], Kz[:, c % 2, g, :], Uz[:, g, :, :].rearrange("p b w -> p (b w)"), start=True, stop=True)
                mm.then_inc(dstate_ready, 1)

            def att_out(s):
                pe.wait_ge(o_ready, s * 1 + 1)
                for m in range(KT_IN):
                    ps = att_use(s, U_OUT + m)
                    for k in range(KT_IN):
                        mm = nc.tensor.matmul(ps[:, :], wout_sb[:, k, m * P:(m + 1) * P], O[:, k * N:(k + 1) * N], start=k == 0, stop=k == KT_IN - 1)
                    mm.then_inc(att_filled, 1)

            def attention(s, e):
                if e == E_MEAN:
                    pe.wait_ge(ffn_added, FFN_V if s is 0 else s * (2 * FFN_V) + 0)
                    sums(s, 0, average, [slab(s)[:, k, :] for k in range(KT_IN)])
                if e == E_VAR:
                    pe.wait_ge(att_squared, s * 1 + 1)
                    sums(s, 1, average, [an[:, k, :] for k in range(KT_IN)])
                for i in range(len(PROJ)):
                    if e == E_PROJ[i]:
                        if i == 0:
                            pe.wait_ge(att_normed, s * KT_IN + KT_IN)
                        project(s, i)
                if e == E_NORM:
                    pe.wait_ge(att_read_s, s * AS + KT_IN)
                    for g in range(KT_IN):
                        sums(s, U_NORM + g, head_ones, [k_sq[:, g * N:(g + 1) * N]])
                if E_KK0 <= e < E_KK0 + 8:
                    for q in range(2 * (e - E_KK0), min(2 * (e - E_KK0) + 2, len(KK))):
                        dots(s, q)
                for c in range(CH):
                    if e == E_RETR[c]:
                        retrieve(s, c)
                    if e == E_STATE[c]:
                        update(s, c)
                    beside = dots_beside(c)
                    if 0 <= e - E_RETR[c] - 2 < len(beside):
                        dots(s, beside[e - E_RETR[c] - 2])
                if 0 <= e - E_QK1 < len(QK):
                    dots(s, DOT_QK[1] + e - E_QK1)
                if e == E_OUT:
                    att_out(s)

            def ln_next(e, call, which):
                if call and e == E_LN[which][0]:
                    ln_mean(call, which == 1)
                if call and e == E_LN[which][1]:
                    ln_var(call)

            def alone(call, first):
                ln_mean(call, first)
                ln_var(call)
                for k in range(SLOTS):
                    if first and k == 48:
                        ln_mean(SECOND, True)
                    if first and k == 54:
                        ln_var(SECOND)
                    ffn(call, k, first)

            def iteration(s, a, b, nxt):
                calls = [c for c in (a, b) if c]
                if s is 0:
                    pe.wait_ge(att_w_loaded, 32)
                for slot in range(SLOTS * len(calls)):
                    for e in events(slot, len(calls)):
                        attention(s, e)
                        if a:
                            ln_next(e, b, 0)
                        ln_next(e, nxt, 1)
                    if not a and slot == 0:
                        ln_mean(b, False)
                        ln_var(b)
                    ffn(calls[slot // SLOTS], slot % SLOTS)

            pe.wait_ge(masks_ready, 3)
            run(pe, alone, iteration)


def kernel(**inputs):
    import numpy as np
    import concourse.bacc as bacc
    from concourse.bass_utils import run_bass_kernel_spmd

    def of(name):
        return np.asarray(inputs["L0_" + name])

    def rows(a):
        return np.ascontiguousarray(a.reshape(-1, P, a.shape[-1]).transpose(1, 0, 2))

    x = of("attn_x").reshape(2, 2, SLABS, CH, C, KT_IN, P)
    x = np.ascontiguousarray(x.transpose(6, 2, 5, 0, 3, 1, 4)).reshape(P, SLABS, KT_IN, N)
    vectors = {"w1_s": "ffn_w1_s", "w2_s": "ffn_w2_s", "h1_s": "ffn_h1_s", "h2_s": "ffn_h2_s", "w3_s": "ffn_w3_s",
               "ln_g": "attn_ln_g", "ln_b": "attn_ln_b", "b_qkvb": "attn_b_qkvb", "b_out": "attn_b_out"}
    weights = {"w1": "ffn_w1_w", "w2": "ffn_w2_w", "h1": "ffn_h1_w", "h2": "ffn_h2_w", "w3": "ffn_w3_w"}
    arrays = {
        "x": x,
        "w": np.ascontiguousarray(np.concatenate([rows(of(weights[n]).T).reshape(P, -1) for n in W_AT], axis=1)),
        "wqkvb": rows(of("attn_w_qkvb")), "wout": rows(of("attn_w_out")),
        "par": np.ascontiguousarray(np.concatenate([of(vectors[n]).reshape(-1, P) for n in PAR]).T),
    }
    nc = bacc.Bacc("TRN2", target_bir_lowering=False, num_devices=1, dynamic_dma_scratch_size=1024)
    args = [nc.dram_tensor(f"in_{n}", list(a.shape), F32, kind="ExternalInput").ap() for n, a in arrays.items()]
    out = nc.dram_tensor("out", list(x.shape), F32, kind="ExternalOutput").ap()
    build(nc, *args, out)
    r = run_bass_kernel_spmd(nc, [{f"in_{n}": a for n, a in arrays.items()}], core_ids=[0])
    y = np.asarray(r.results[0]["out"]).reshape(P, SLABS, KT_IN, 2, CH, 2, C)
    return np.ascontiguousarray(y.transpose(3, 5, 1, 4, 6, 2, 0)).reshape(B, T, HID)
```

```python
from contextlib import ExitStack

import concourse.bass as bass
from concourse import mybir

F32 = mybir.dt.float32
F16 = mybir.dt.float16
ALU = mybir.AluOpType
ACT = mybir.ActivationFunctionType
AX = mybir.AxisListType

P = 128
B, T, HID = 4, 1024, 256
NH, D = 16, 16
FF = 1024
LN_EPS = 1e-5
NORM_EPS = 1e-6

KT_IN = HID // P
KT_FF = FF // P
SLAB_T = 128
SLABS = T // SLAB_T
N = B * SLAB_T
C = 16
CH = SLAB_T // C
HP = P // D
QUADS = P // 32
GB = KT_IN * B
GP = GB // 2
ITEMS = GP * CH
RUNS = 2 * ITEMS
COLS = KT_IN * N
HALVES = 2
HCH = CH // HALVES
HRUNS = RUNS // HALVES
RING = 4

PAR = {}
for _name, _n in (("w1_s", KT_FF), ("w2_s", KT_FF), ("h1_s", KT_FF), ("h2_s", KT_FF), ("w3_s", KT_IN),
                  ("ln_g", KT_IN), ("ln_b", KT_IN), ("b_qkvb", 4 * KT_IN), ("b_out", KT_IN)):
    PAR[_name] = (sum(n for _, n in PAR.values()), _n)
NPAR = sum(n for _, n in PAR.values())

W_AT = {}
for _name, _n in (("w1", KT_IN * FF), ("w2", KT_IN * FF), ("h1", KT_FF * FF), ("h2", KT_FF * FF), ("w3", KT_FF * HID)):
    W_AT[_name] = (sum(n for _, n in W_AT.values()), _n)
W_COLS = sum(n for _, n in W_AT.values())
W_PIECE = 2048
W_PIECES = W_COLS // W_PIECE
W_STAGES = 3
W_DONE = {name: -(-(at + n) // W_PIECE) for name, (at, n) in W_AT.items()}

KK = [(t, t) for t in range(1, C)]
QK = [(t, t + 1) for t in range(C)]
KK_AT = [HRUNS * t * (t - 1) // 2 for t in range(C + 1)]
DOTS = HALVES * (len(KK) + len(QK))
DOT_KK = [h * len(KK) for h in range(HALVES)]
DOT_QK = [HALVES * len(KK) + h * len(QK) for h in range(HALVES)]
SPLITS = DOT_QK[1] - DOT_KK[1]
PAIR_BUFFERS, HALF_BUFFERS = 4, 3

L2, L3, LO = 2 * KT_FF, 2 * KT_FF + 4 * KT_FF, 2 * KT_FF + 8 * KT_FF
SLOTS = LO + KT_FF
FFN_BANKS = 4
FFN_S, FFN_V = 4 * KT_FF, KT_IN
FFN_U = FFN_S + FFN_V
UNITS = 3 * KT_FF

ATT_BANKS = 2
PROJ = [2, 3, 0, 1, 6, 7, 4, 5]
ATT_USES = "SSSS" + "VV" + "SSSS" + "V" * DOTS + "VV"
U_PROJ = [0, 1, 2, 3, 6, 7, 8, 9]
U_NORM = 4
U_DOTS = 10
U_OUT = U_DOTS + DOTS
ATT_U = len(ATT_USES)
AV, AS = ATT_USES.count("V"), ATT_USES.count("S")

STEP_KNORM = 1
CHUNK_STEPS = 2 + 2 * (C - 1) + 1
ATT_STEPS = STEP_KNORM + CH * CHUNK_STEPS + 1

TICKS = 2 * SLOTS
ACT_LAG, POOL_LAG = 2, 3
E_PROJ = [2, 3, 4, 5, 8, 9, 10, 11]
E_NORM, E_KROOT = 7, 10
E_RETR = [14] + [29 + 16 * c for c in range(CH - 1)]
E_STATE = [E_RETR[0] + 13] + [e + 14 for e in E_RETR[1:]]
E_OUT = 160
LN_B = dict(sum=11, mean=12, square=15, sq_sum=16, var=19, root=25, apply=45, low=47)
LN_NEXT = dict(sum=50, mean=53, square=61, sq_sum=62, var=65, root=109, apply=125, low=127)
LN_ATT = dict(sum=129, mean=131, square=142, sq_sum=143, var=146, root=164, apply=168, y_root=172, low=174)
LN_ATT_FIRST = dict(sum=-18, mean=-15, square=-13, sq_sum=-11, var=-9, root=-4, apply=-2, y_root=4, low=8)
LN_LAST = dict(sum=0, mean=2, square=4, sq_sum=5, var=6, root=8, apply=13, low=13)
LN_SECOND = dict(sum=46, mean=48, square=50, sq_sum=51, var=54, root=60, apply=70, y_root=75, low=80)
QUARTERS = 4
SOLVE_B = {8: "offset", 9: 0, 10: 1, 11: 2, 12: 3}
BESIDE_B = {(1, "d"): "norm"}
BESIDE_NEXT = {(2, "d"): "center", (3, "d"): "offset", (3, "r"): 0, (4, "d"): 1, (4, "r"): 2, (5, "d"): 3, (6, "d"): "norm"}
BESIDE_ATT = {(7, "d"): "center"}
OUT_CHUNK, OUT_STEP = 4, 15

BOTH, ONE_FIRST, ONE_LAST = (TICKS, 0, 1, 1), (SLOTS, -18, 20, 18), (SLOTS, 0, 1, 17)


def ticks_of(slot, kind):
    slots, start, head_slots, head_ticks = kind

    def upto(x):
        if x <= head_slots:
            return start + x * head_ticks // head_slots
        rest = TICKS - start - head_ticks
        return start + head_ticks + (x - head_slots) * rest // (slots - head_slots)
    return range(upto(slot), upto(slot + 1))


def is_zero(v):
    return isinstance(v, int) and v == 0


def reads(who, j):
    return ATT_USES[:j + 1].count(who)


def dots_beside(c):
    if 1 <= c < HCH:
        return range(DOT_KK[1] + 5 * (c - 1), DOT_KK[1] + 5 * c)
    if c >= HCH:
        return range(DOT_QK[0] + 4 * (c - HCH), DOT_QK[0] + 4 * (c - HCH) + 4)
    return range(0)


TAKE_STEPS = range(6, C, 2)

PAIR_LEAD = {False: 4, True: 6}
HIGH_LEAD, LOW_LEAD = 4, 3
DOT_TICK = {DOT_KK[0] + i: E_RETR[0] + 2 + 2 * i // 3 for i in range(len(KK))}
for _c in range(CH):
    DOT_TICK.update({q: E_RETR[_c] + 3 + 3 * i // 2 for i, q in enumerate(dots_beside(_c))})
DOT_TICK.update({DOT_QK[1] + i: E_STATE[-1] + 2 + i for i in range(len(QK))})


def is_split(q):
    return DOT_KK[1] <= q < DOT_QK[1]


def dots_at(tick, split=None):
    return [q for q, e in DOT_TICK.items() if e == tick and split in (None, is_split(q))]


def dot(q):
    if q < DOT_QK[0]:
        h, j = divmod(q, len(KK))
        return (False, h) + KK[j]
    h, j = divmod(q - DOT_QK[0], len(QK))
    return (True, h) + QK[j]


def build(nc, x, w, wqkvb, wout, par, out):
    with ExitStack() as ctx:
        def sb(name, shape, dt=F32):
            return ctx.enter_context(nc.sbuf_tensor(name, shape, dt))

        def bank(name):
            return ctx.enter_context(nc.psum_tensor(name, [P, 512], F32))

        def sem(name):
            return ctx.enter_context(nc.semaphore(name))

        w_sb = sb("w_sb", [P, W_COLS], F16)
        wqkvb_sb = sb("wqkvb_sb", [P, KT_IN, 4 * HID])
        wout_sb = sb("wout_sb", [P, KT_IN, HID])
        par_sb = sb("par_sb", [P, NPAR])
        w3_half = sb("w3_half", [P, KT_IN])
        ln_gain = sb("ln_gain", [P, KT_IN])
        average = sb("average", [P, P])
        head_ones = sb("head_ones", [P, P])
        head_minus = sb("head_minus", [P, P])
        head_ones16 = sb("head_ones16", [P, P], F16)
        head_minus16 = sb("head_minus16", [P, P], F16)
        quad_ones = sb("quad_ones", [P, QUADS])
        side_ones = sb("side_ones", [P, 2])
        X = sb("X", [P, RING, KT_IN, N])
        xc = sb("xc", [P, KT_IN, N])
        xn = sb("xn", [P, KT_IN, N])
        roots = sb("roots", [P, 2, N])
        feature_sum = roots[:, 1, :]
        xn_hi = sb("xn_hi", [P, KT_IN, N], F16)
        xn_lo = sb("xn_lo", [P, KT_IN, N], F16)
        gate = sb("gate", [P, 2, N])
        hid = sb("hid", [P, 3, N])
        hid_hi = [sb(f"hid_hi{i}", [P, KT_FF, N], F16) for i in range(2)]
        hid_lo = [sb(f"hid_lo{i}", [P, KT_FF, N], F16) for i in range(2)]
        KQ = sb("KQ", [P, 2, COLS])
        V = sb("V", [P, COLS])
        beta = sb("beta", [P, COLS])
        U = sb("U", [P, COLS])
        O = sb("O", [P, COLS])
        k_sq = O
        O_in = sb("O_in", [P, COLS])
        k_raw = O_in
        NK = sb("NK", [P, HALVES, KK_AT[C]])
        stage = NK[:, :, :].rearrange("p h n -> p (h n)")
        pairs = sb("pairs", [P, PAIR_BUFFERS, N])
        pairs_hi = sb("pairs_hi", [P, HALF_BUFFERS, N], F16)
        pairs_lo = sb("pairs_lo", [P, HALF_BUFFERS, N], F16)
        qk_u = sb("qk_u", [P, N])
        KTr = sb("KTr", [P, 2, GP, 32])
        Kz = sb("Kz", [P, GP, P])
        UTr = sb("UTr", [P, GP, 32])
        Uz = sb("Uz", [P, GP, 2, 32])
        terms = sb("terms", [P, C, GB, C])
        resid = sb("resid", [P, GB, C])
        state = sb("state", [P, GB, 32])
        state_bd = sb("state_bd", [P, GB, P])

        ffn_bank = [bank(f"ffn_bank{i}") for i in range(FFN_BANKS)]
        ln_bank = bank("ln_bank")
        att_bank = [bank(f"att_bank{i}") for i in range(ATT_BANKS)]
        state_bank = bank("state_bank")
        retr_ps = state_bank[:, 0:GB * 2 * C]
        dstate_ps = state_bank[:, 256:512]

        x_loaded, par_loaded, att_w_loaded, w_staged, stored = (sem(n) for n in (
            "x_loaded", "par_loaded", "att_w_loaded", "w_staged", "stored"))
        masks_step, masks_ready, side_ready, consts_ready, state_zeroed, w_ready = (sem(n) for n in (
            "masks_step", "masks_ready", "side_ready", "consts_ready", "state_zeroed", "w_ready"))
        ln_summed, ln_filled, ln_read, ln_squared, ln_sq_summed, ln_inverted, ln_rooted, ln_normed = (sem(n) for n in (
            "ln_summed", "ln_filled", "ln_read", "ln_squared", "ln_sq_summed", "ln_inverted", "ln_rooted", "ln_normed"))
        ln_hi, ln_lo = sem("ln_hi"), sem("ln_lo")
        ffn_filled, ffn_read, ffn_added = sem("ffn_filled"), sem("ffn_read"), sem("ffn_added")
        hid_mixed, hid_hi_ready, hid_lo_ready = sem("hid_mixed"), sem("hid_hi_ready"), sem("hid_lo_ready")
        att_filled, att_read_v, att_read_s = sem("att_filled"), sem("att_read_v"), sem("att_read_s")
        att_offset, att_normed, k_rooted, y_inverted, y_rooted = (sem(n) for n in (
            "att_offset", "att_normed", "k_rooted", "y_inverted", "y_rooted"))
        y_scaled, y_added, k_ready, k_turned, pairs_made, pairs_hi_ready, pairs_ready, kz_ready = (sem(n) for n in (
            "y_scaled", "y_added", "k_ready", "k_turned", "pairs_made", "pairs_hi_ready", "pairs_ready", "kz_ready"))
        retr_ready, resid_ready, q_saved, u_turned, u_ready, dstate_ready, state_ready = (sem(n) for n in (
            "retr_ready", "resid_ready", "q_saved", "u_turned", "u_ready", "dstate_ready", "state_ready"))
        att_step, o_ready = sem("att_step"), sem("o_ready")

        def p(name, j):
            a = PAR[name][0] + j
            return par_sb[:, a:a + 1]

        def weight(name, k, m):
            at, n = W_AT[name]
            width = HID if name == "w3" else FF
            a = at + k * width + m * P
            return w_sb[:, a:a + P]

        def slab(s):
            return X[:, bass.ds(s % RING, 1), :, :].rearrange("p s k n -> p (s k) n")

        def both(ap):
            return ap.unsqueeze(1).to_broadcast([P, KT_IN, N])

        def half(ap, h):
            return ap.rearrange("p (g h r t) -> p g h r t", h=HALVES, r=2 * HCH, t=C)[:, :, h, :, :]

        def at_chunk(ap, c):
            return ap.rearrange("p (g c b t) -> p g c b t", c=CH, b=2, t=C)[:, :, c, :, :]

        def packed(ap, n):
            return ap.rearrange("p (g r w) -> p g r w", g=GP, w=n)

        def nk_row(t, c):
            row = NK[:, c // HCH, KK_AT[t]:KK_AT[t + 1]]
            return row.rearrange("p (g c b t) -> p g c b t", c=HCH, b=2, t=t)[:, :, c % HCH, :, :]

        def four(ap):
            return ap.rearrange("p (g b) t -> p g b t", b=2)

        def ffn_ps(off, j):
            return ffn_bank[(off + j) % FFN_BANKS][:, :]

        def pair(buf, q):
            w = dot(q)[3]
            return buf[:, q % buf.shape[1], 0:HRUNS * w]

        block = ctx.enter_context(nc.Block())

        FIRST, SECOND = (0, 0, 0), (1, 2, 1)
        LAST2, LAST = (2 * SLABS - 2, 0, SLABS - 2), (2 * SLABS - 1, 2, SLABS - 1)

        def calls_of(s):
            return (s * 2, 0, s + 1), (s * 2 + 1, 2, s - 1)

        def run(eng, alone, iteration, norm_only):
            second = (1, 1, "ffn1", 1, 0)
            alone(FIRST, (0, 0, "ffn1", 0, 0), second)
            iteration(0, ONE_FIRST, SECOND, None, ((2, 0, "att", None, 0), None, (3, 2, "ffn1", 2, 1), None))
            norm_only((4, 1, "att", None, 1))
            with eng.Fori(1, SLABS - 2) as s:
                a, b = calls_of(s)
                iteration(s, BOTH, a, b, (None, (s * 3 + 2, s - 1, "ffn2", b[0], s + 1), (s * 3 + 3, s + 2, "ffn1", s * 2 + 2, s + 1),
                                          (s * 3 + 4, s + 1, "att", None, s + 1)))
            s = SLABS - 2
            a, b = calls_of(s)
            iteration(s, BOTH, a, b, (None, (s * 3 + 2, s - 1, "ffn2", b[0], s + 1), None, (s * 3 + 3, s + 1, "att", None, s + 1)))
            iteration(s + 1, ONE_LAST, None, LAST2, (None, (s * 3 + 4, s, "ffn2", LAST2[0], s + 2), None, None))
            alone(LAST, (s * 3 + 5, s + 1, "ffn2", LAST[0], s + 2), None)

        def squares(job):
            ys = job[4]
            return gate if isinstance(ys, int) and ys == SLABS else xn

        def in_order(s, kind, a, b, jobs, attention, ln, ffn, lag=0):
            calls = [c for c in (a, b) if c]
            for slot in range(kind[0]):
                for tick in ticks_of(slot, kind):
                    for job, at in zip(jobs, (LN_ATT_FIRST, LN_B if a else LN_LAST, LN_NEXT, LN_ATT)):
                        if job:
                            for part in [p for p, e in at.items() if e == tick]:
                                ln(part, job)
                    attention(s, tick)
                k = slot - lag
                if k >= 0:
                    ffn(calls[k // SLOTS], k % SLOTS)

        def whole_norm(job, ln):
            for part in LN_SECOND:
                ln(part, job)

        def by_itself(call, job, second, ln, ffn, lag=0):
            whole_norm(job, ln)
            for k in range(SLOTS):
                if second:
                    for part in [p for p, e in LN_SECOND.items() if e == k]:
                        ln(part, second)
                if k >= lag:
                    ffn(call, k - lag)

        @block.sync
        def _(sp):
            def load(s, slot):
                sp.dma_start(X[:, bass.ds(slot, 1), :, :], x[:, bass.ds(s, 1), :, :]).then_inc(x_loaded, 16)

            def store(s, slot):
                sp.dma_start(out[:, bass.ds(s, 1), :, :], X[:, bass.ds(slot, 1), :, :]).then_inc(stored, 16)

            def stage_piece(i):
                if i >= W_STAGES:
                    sp.wait_ge(w_ready, i - W_STAGES + 1)
                a = i % W_STAGES * W_PIECE
                sp.dma_start(stage[:, a:a + W_PIECE], w[:, i * W_PIECE:(i + 1) * W_PIECE]).then_inc(w_staged, 16)
                sp.wait_ge(w_staged, 16 * (i + 1))

            sp.dma_start(par_sb[:, :], par).then_inc(par_loaded, 16)
            load(0, 0)
            sp.wait_ge(x_loaded, 16)
            for i in range(W_PIECES):
                stage_piece(i)
                if i == 2:
                    load(1, 1)
            sp.dma_start(wqkvb_sb[:, :, :], wqkvb).then_inc(att_w_loaded, 16)
            sp.dma_start(wout_sb[:, :, :], wout).then_inc(att_w_loaded, 16)
            for s in range(2, RING):
                sp.wait_ge(x_loaded, 16 * s)
                load(s, s)
            with sp.Fori(0, SLABS - RING) as s:
                sp.wait_ge(ffn_added, (s * 2 + 4) * FFN_V)
                store(s, s % RING)
                sp.wait_ge(stored, (s + 1) * 16)
                sp.wait_ge(x_loaded, s * 16 + 16 * RING)
                load(s + RING, s % RING)
            for s in range(SLABS - RING, SLABS):
                sp.wait_ge(ffn_added, ((2 * s + 3 if s < SLABS - 2 else SLABS + s) + 1) * FFN_V)
                store(s, s % RING)
            sp.wait_ge(stored, 16 * SLABS)

        @block.gpsimd
        def _(pool):
            pool.memset(average[:, :], 1.0 / HID).then_inc(masks_ready, 1)
            pool.memset(head_ones[:, :], 1.0).then_inc(masks_step, 1)
            pool.wait_ge(masks_step, 1)
            view = head_ones[:, :].rearrange("p (h i) -> p h i", i=D)
            pool.affine_select(out=view, in_=view, compare_op=ALU.is_ge, fill=0.0, base=0,
                               pattern=[[-D, HP], [0, D]], channel_multiplier=1).then_inc(masks_step, 1)
            pool.wait_ge(masks_step, 2)
            pool.affine_select(out=view, in_=view, compare_op=ALU.is_ge, fill=0.0, base=D - 1,
                               pattern=[[D, HP], [0, D]], channel_multiplier=-1).then_inc(masks_ready, 1)
            pool.memset(state[:, :, :], 0.0).then_inc(state_zeroed, 1)
            pool.memset(state_bd[:, :, :], 0.0).then_inc(state_ready, 1)
            pool.wait_ge(side_ready, 5)

            def ln(part, job):
                i, s, kind, n, _ = job
                if part == "sum":
                    if kind == "ffn1":
                        pool.wait_ge(x_loaded, s * 16 + 16)
                    elif kind == "ffn2":
                        pool.wait_ge(att_read_v, (s + 1) * AV)
                    else:
                        pool.wait_ge(ffn_added, (s + 1) * FFN_V if isinstance(s, int) and s < 2 else (s * 2 - 1) * FFN_V)
                    if not is_zero(i):
                        pool.wait_ge(ln_normed, i * 1)
                    pool.tensor_tensor(feature_sum.unsqueeze(1), slab(s)[:, 0:1, :], slab(s)[:, 1:2, :], ALU.add).then_inc(ln_summed, 1)
                if part == "sq_sum":
                    pool.wait_ge(ln_squared, i * 1 + 1)
                    sq = squares(job)
                    pool.tensor_tensor(feature_sum, sq[:, 0, :], sq[:, 1, :], ALU.add).then_inc(ln_sq_summed, 1)
                if part == "low" and kind != "att":
                    pool.wait_ge(ln_hi, n * 1 + 1)
                    pool.tensor_tensor(xn_lo[:, :, :], xn[:, :, :], xn_hi[:, :, :], ALU.subtract).then_inc(ln_lo, 1)
                if part == "low" and kind == "att":
                    pool.wait_ge(y_rooted, s * 1 + 1)
                    pool.tensor_tensor(xc[:, :, :], xc[:, :, :], both(roots[:, 0, :]), ALU.mult).then_inc(y_scaled, 1)
                    pool.wait_ge(y_scaled, s * 1 + 1)
                    resid = slab(s + RING)
                    pool.tensor_tensor(resid, resid, xc[:, :, :], ALU.add).then_inc(y_added, 1)

            def low(n, u):
                layer, m = divmod(u, KT_FF)
                pool.wait_ge(hid_hi_ready, n * UNITS + (u + 1))
                pool.tensor_tensor(hid_lo[layer % 2][:, m, :], hid[:, u % 3, :], hid_hi[layer % 2][:, m, :],
                                   ALU.subtract).then_inc(hid_lo_ready, 1)

            def ffn(call, k):
                n, _, _ = call
                if k < L2 and k % 2:
                    m = k // 2
                    pool.wait_ge(ffn_read, n * FFN_S + (2 * m + 2))
                    pool.tensor_tensor(hid[:, m % 3, :], hid[:, m % 3, :], gate[:, m % 2, :], ALU.mult).then_inc(hid_mixed, 1)
                    if m >= 1:
                        low(n, m - 1)
                elif k == L2:
                    low(n, KT_FF - 1)
                elif L2 <= k < LO and k % 8 == 7:
                    u = KT_FF + (k - L2) // 8 * 2
                    low(n, u)
                    low(n, u + 1)

            def make_pairs(s, q):
                of_q, h, t, w = dot(q)
                if q == 0:
                    pool.wait_ge(k_ready, s * KT_IN + KT_IN)
                if q >= PAIR_BUFFERS:
                    if is_split(q - PAIR_BUFFERS):
                        pool.wait_ge(pairs_ready, s * DOTS + (q - PAIR_BUFFERS + 1))
                    else:
                        pool.wait_ge(att_filled, s * ATT_U + (U_DOTS + q - PAIR_BUFFERS + 1))
                later = half(KQ[:, 1 if of_q else 0, :], h)[:, :, :, t:t + 1].to_broadcast([P, GP, 2 * HCH, w])
                pool.tensor_tensor(packed(pair(pairs, q), w), later, half(KQ[:, 0, :], h)[:, :, :, 0:w], ALU.mult).then_inc(pairs_made if is_split(q) else pairs_ready, 1)

            def low_pairs(s, q):
                pool.wait_ge(pairs_hi_ready, s * SPLITS + (q - DOT_KK[1] + 1))
                if is_split(q - HALF_BUFFERS):
                    pool.wait_ge(att_filled, s * ATT_U + (U_DOTS + q - HALF_BUFFERS + 1))
                pool.tensor_tensor(pair(pairs_lo, q), pair(pairs, q), pair(pairs_hi, q), ALU.subtract).then_inc(pairs_ready, 1)

            def make_kz(s, c):
                if c >= 1:
                    pool.wait_ge(dstate_ready, s * CH + c)
                pool.wait_ge(k_turned, s * CH + (c + 1))
                keys = KTr[:, c % 2, :, :].unsqueeze(2)
                pool.tensor_tensor(Kz[:, :, :].rearrange("p g (q w) -> p g q w", w=32),
                                   keys.to_broadcast([P, GP, QUADS, 32]),
                                   quad_ones[:, :].unsqueeze(1).unsqueeze(3).to_broadcast([P, GP, QUADS, 32]),
                                   ALU.mult).then_inc(kz_ready, 1)

            def attention(s, e):
                for q in dots_at(e + LOW_LEAD, True):
                    low_pairs(s, q)
                for split, lead in PAIR_LEAD.items():
                    for q in dots_at(e + lead, split):
                        make_pairs(s, q)
                for c in range(CH):
                    if e == E_RETR[c] + 6:
                        make_kz(s, c)

            def alone(call, job, second):
                by_itself(call, job, second, ln, ffn, POOL_LAG)

            def iteration(s, kind, a, b, jobs):
                in_order(s, kind, a, b, jobs, attention, ln, ffn, POOL_LAG)

            run(pool, alone, iteration, lambda job: whole_norm(job, ln))

        @block.scalar
        def _(act):
            act.wait_ge(par_loaded, 16)
            act.mul(w3_half[:, :], par_sb[:, PAR["w3_s"][0]:PAR["w3_s"][0] + KT_IN], 0.5).then_inc(consts_ready, 1)
            act.mul(ln_gain[:, :], par_sb[:, PAR["ln_g"][0]:PAR["ln_g"][0] + KT_IN],
                    (1.0 + LN_EPS) ** -0.5).then_inc(consts_ready, 1)
            act.wait_ge(consts_ready, 2)

            def ln(part, job):
                i, s, kind, _, _ = job
                if part == "square":
                    act.wait_ge(ln_read, i * 2 + 1)
                    sq = squares(job)
                    act.activation(sq[:, :, :], xc[:, :, :], ACT.Square).then_inc(ln_squared, 1)
                if part == "root":
                    act.wait_ge(ln_inverted, i * 1 + 1)
                    r = roots[:, 1 if kind == "att" else 0, :]
                    act.activation(r, r, ACT.Sqrt).then_inc(ln_rooted, 1)
                if part == "y_root" and kind == "att":
                    act.wait_ge(y_inverted, s * 1 + 1)
                    act.activation(roots[:, 0, :], roots[:, 0, :], ACT.Sqrt).then_inc(y_rooted, 1)
                if part == "apply":
                    act.wait_ge(ln_normed, i * 1 + 1)
                    if kind == "att":
                        for k in range(KT_IN):
                            act.activation(xn[:, k, :], xn[:, k, :], ACT.Identity, scale=ln_gain[:, k:k + 1],
                                           bias=p("ln_b", k)).then_inc(att_normed, 1)
                    else:
                        act.copy(xn_hi[:, :, :], xn[:, :, :]).then_inc(ln_hi, 1)

            def high(n, u):
                layer, m = divmod(u, KT_FF)
                if u < KT_FF:
                    act.wait_ge(hid_mixed, n * KT_FF + (u + 1))
                act.copy(hid_hi[layer % 2][:, m, :], hid[:, u % 3, :]).then_inc(hid_hi_ready, 1)

            def ffn(call, k):
                n, off, _ = call
                if k < L2:
                    m = k // 2
                    act.wait_ge(ffn_filled, n * FFN_U + (k + 1))
                    if k % 2 == 0:
                        if m >= 2:
                            act.wait_ge(hid_mixed, n * KT_FF + (m - 1))
                        act.activation(gate[:, m % 2, :], ffn_ps(off, k), ACT.Silu, scale=p("w1_s", m)).then_inc(ffn_read, 1)
                    else:
                        if m >= 3:
                            act.wait_ge(hid_lo_ready, n * UNITS + (m - 2))
                        act.activation(hid[:, m % 3, :], ffn_ps(off, k), ACT.Copy, scale=p("w2_s", m)).then_inc(ffn_read, 1)
                        if m >= 1:
                            high(n, m - 1)
                elif k == L2:
                    high(n, KT_FF - 1)
                elif L2 <= k < LO and k % 8 == 7:
                    u = KT_FF + (k - L2) // 8 * 2
                    for i in range(2):
                        j = KT_FF + u + i
                        layer, m = divmod(u + i, KT_FF)
                        act.wait_ge(ffn_filled, n * FFN_U + (j + 1))
                        act.wait_ge(hid_lo_ready, n * UNITS + (u + i - 2))
                        act.activation(hid[:, (u + i) % 3, :], ffn_ps(off, j), ACT.Gelu,
                                       scale=p(("h1_s", "h2_s")[layer - 1], m)).then_inc(ffn_read, 1)
                    for i in range(2):
                        act.wait_ge(ffn_read, n * FFN_S + (KT_FF + u + i + 1))
                        high(n, u + i)

            def project(s, i):
                j, use = PROJ[i], U_PROJ[i]
                which, g = divmod(j, KT_IN)
                cols = slice(g * N, (g + 1) * N)
                ps = att_bank[use % ATT_BANKS][:, :]
                dest = (KQ[:, 1, cols], k_raw[:, cols], V[:, cols], beta[:, cols])[which]
                act.wait_ge(att_filled, s * ATT_U + (use + 1))
                if which == 1:
                    act.activation(k_sq[:, cols], ps, ACT.Square, bias=p("b_qkvb", j))
                act.activation(dest, ps, ACT.Sigmoid if which == 3 else ACT.Identity, bias=p("b_qkvb", j)).then_inc(att_read_s, 1)

            def high_pairs(s, q):
                act.wait_ge(pairs_made, s * SPLITS + (q - DOT_KK[1] + 1))
                if is_split(q - HALF_BUFFERS):
                    act.wait_ge(att_filled, s * ATT_U + (U_DOTS + q - HALF_BUFFERS + 1))
                act.copy(pair(pairs_hi, q), pair(pairs, q)).then_inc(pairs_hi_ready, 1)

            def attention(s, e):
                for q in dots_at(e + HIGH_LEAD, True):
                    high_pairs(s, q)
                for i in range(len(PROJ)):
                    if e == E_PROJ[i] + 1:
                        project(s, i)
                if e == E_KROOT:
                    act.wait_ge(att_step, s * ATT_STEPS + STEP_KNORM)
                    act.activation(k_sq[:, :], k_sq[:, :], ACT.Sqrt).then_inc(k_rooted, 1)
                for c in range(CH):
                    if e == E_RETR[c] + 5:
                        act.wait_ge(resid_ready, s * CH + (c + 1))
                        act.copy(at_chunk(O[:, :], c), four(retr_ps.rearrange("p (g w) -> p g w", w=2 * C)[:, :, C:2 * C])).then_inc(q_saved, 1)

            def alone(call, job, second):
                by_itself(call, job, second, ln, ffn, ACT_LAG)

            def iteration(s, kind, a, b, jobs):
                in_order(s, kind, a, b, jobs, attention, ln, ffn, ACT_LAG)

            run(act, alone, iteration, lambda job: whole_norm(job, ln))

        @block.vector
        def _(dve):
            dve.wait_ge(masks_ready, 2)
            of_head = head_ones[:, :].rearrange("p (q b w) -> p q b w", b=2, w=D)[:, :, :, 0]
            nc.vector.tensor_reduce(quad_ones[:, :], of_head, AX.X, ALU.add).then_inc(side_ready, 1)
            nc.vector.tensor_reduce(side_ones[:, :], of_head.rearrange("p q b -> p b q"), AX.X, ALU.add).then_inc(side_ready, 1)
            nc.vector.tensor_scalar(head_minus[:, :], head_ones[:, :], -1.0, None, ALU.mult).then_inc(side_ready, 1)
            nc.vector.tensor_copy(head_ones16[:, :], head_ones[:, :]).then_inc(side_ready, 1)
            nc.vector.tensor_scalar(head_minus16[:, :], head_ones[:, :], -1.0, None, ALU.mult).then_inc(side_ready, 1)
            dve.wait_ge(consts_ready, 2)
            dve.wait_ge(state_zeroed, 1)
            dve.wait_ge(side_ready, 5)

            def convert(i):
                a = i % W_STAGES * W_PIECE
                dve.wait_ge(w_staged, 16 * (i + 1))
                nc.vector.tensor_copy(w_sb[:, i * W_PIECE:(i + 1) * W_PIECE], stage[:, a:a + W_PIECE]).then_inc(w_ready, 1)

            def ln_center(job):
                i, s, _, _, ys = job
                if not is_zero(ys):
                    dve.wait_ge(y_added, ys * 1)
                dve.wait_ge(ln_filled, i * 2 + 1)
                nc.vector.tensor_tensor(xc[:, :, :], slab(s), both(ln_bank[:, :]), ALU.subtract).then_inc(ln_read, 1)

            def ln_offset(job):
                i, s, kind, _, _ = job
                dve.wait_ge(ln_filled, i * 2 + 2)
                if kind == "att":
                    nc.vector.tensor_scalar(roots[:, 1, :], ln_bank[:, :], LN_EPS * LN_EPS / (1 + LN_EPS), None, ALU.add).then_inc(att_offset, 1)
                nc.vector.tensor_scalar(roots[:, 0, :], ln_bank[:, :], LN_EPS, None, ALU.add).then_inc(ln_read, 1)

            def ln_recip(job, quarter=None):
                i, s, kind, _, _ = job
                if not quarter:
                    if kind == "att":
                        dve.wait_ge(att_offset, s * 1 + 1)
                    else:
                        dve.wait_ge(ln_read, i * 2 + 2)
                r = roots[:, 1 if kind == "att" else 0, :]
                if quarter is not None:
                    r = r[:, quarter * N // QUARTERS:(quarter + 1) * N // QUARTERS]
                done = nc.vector.reciprocal(r, r)
                if quarter in (None, QUARTERS - 1):
                    done.then_inc(ln_inverted, 1)

            def ln_invert(job):
                ln_offset(job)
                ln_recip(job)

            def ln_part(job, part):
                if isinstance(part, str):
                    dict(center=ln_center, offset=ln_offset, invert=ln_invert, norm=ln_norm)[part](job)
                else:
                    ln_recip(job, part)

            def ln_norm(job):
                i, s, kind, _, ys = job
                dve.wait_ge(ln_rooted, i * 1 + 1)
                if not is_zero(ys):
                    dve.wait_ge(att_read_s, ys * AS)
                r = roots[:, 1 if kind == "att" else 0, :]
                nc.vector.tensor_tensor(xn[:, :, :], xc[:, :, :], both(r), ALU.mult).then_inc(ln_normed, 1)
                if kind == "att":
                    dve.wait_ge(ln_read, i * 2 + 2)
                    nc.vector.reciprocal(roots[:, 0, :], roots[:, 0, :]).then_inc(y_inverted, 1)

            def ffn_out(call):
                n, off, s = call
                xs = slab(s)
                for m in range(KT_IN):
                    j = FFN_S + m
                    dve.wait_ge(ffn_filled, n * FFN_U + (j + 1))
                    nc.vector.scalar_tensor_tensor(xs[:, m, :], ffn_ps(off, j), w3_half[:, m:m + 1],
                                                   xs[:, m, :], ALU.mult, ALU.add).then_inc(ffn_added, 1)

            def use(s, j):
                dve.wait_ge(att_filled, s * ATT_U + (j + 1))
                return att_bank[j % ATT_BANKS]

            def key_invert(s):
                for g in range(KT_IN):
                    ps = use(s, U_NORM + g)
                    nc.vector.tensor_scalar(k_sq[:, g * N:(g + 1) * N], ps[:, :], NORM_EPS * NORM_EPS, None, ALU.max).then_inc(att_read_v, 1)
                dve.wait_ge(att_read_v, s * AV + reads("V", U_NORM + 1))
                nc.vector.reciprocal(k_sq[:, :], k_sq[:, :]).then_inc(att_step, 1)

            def key_scale(s):
                dve.wait_ge(k_rooted, s * 1 + 1)
                for g in range(KT_IN):
                    cols = slice(g * N, (g + 1) * N)
                    nc.vector.tensor_tensor(KQ[:, 0, cols], k_raw[:, cols], k_sq[:, cols], ALU.mult).then_inc(k_ready, 1)
                dve.wait_ge(k_ready, s * KT_IN + KT_IN)

            def take_dots(s, q):
                of_q, h, t, w = dot(q)
                ps = packed(use(s, U_DOTS + q)[:, 0:HRUNS * w], w)
                if not of_q:
                    nc.vector.tensor_tensor(packed(NK[:, h, KK_AT[t]:KK_AT[t + 1]], w), ps,
                                            half(beta[:, :], h)[:, :, :, t:t + 1].to_broadcast([P, GP, 2 * HCH, w]),
                                            ALU.mult).then_inc(att_read_v, 1)
                    return
                buf = half(V[:, :], 0)[:, :, :, 0:w] if q % 2 else packed(qk_u[:, 0:HRUNS * w], w)
                nc.vector.tensor_tensor(buf, ps, half(U[:, :], h)[:, :, :, 0:w], ALU.mult).then_inc(att_read_v, 1)
                dve.wait_ge(att_read_v, s * AV + reads("V", U_DOTS + q))
                summed = nc.vector.tensor_reduce(half(O_in[:, :], h)[:, :, :, t], buf, AX.X, ALU.add)
                if q == DOTS - 1:
                    summed.then_inc(att_step, 1)

            def chunk(s, c, beside, call, job):
                count = [STEP_KNORM + c * CHUNK_STEPS]

                def step(ins):
                    count[0] += 1
                    ins.then_inc(att_step, 1)

                def last_step():
                    dve.wait_ge(att_step, s * ATT_STEPS + count[0])

                if c == HCH:
                    dve.wait_ge(att_read_v, s * AV + reads("V", U_DOTS + DOT_KK[c // HCH] + len(KK) - 1))
                if c == 0:
                    dve.wait_ge(att_read_s, s * AS + AS)
                    dve.wait_ge(y_added, s * 1 + 1)
                dots = list(dots_beside(c))
                if c >= 2:
                    dve.wait_ge(kz_ready, s * CH + (c - 1))
                nc.vector.transpose(KTr[:, c % 2, :, :], at_chunk(KQ[:, 0, :], c).rearrange("p g b t -> p g (b t)")).then_inc(k_turned, 1)
                dve.wait_ge(retr_ready, s * CH + (c + 1))
                retr = retr_ps.rearrange("p (g w) -> p g w", w=2 * C)[:, :, 0:C]
                nc.vector.tensor_tensor(four(resid[:, :, :]), at_chunk(V[:, :], c), four(retr), ALU.subtract).then_inc(resid_ready, 1)
                dve.wait_ge(resid_ready, s * CH + (c + 1))
                heads = terms[:, :, :, 0].rearrange("p t g -> p g t")
                step(nc.vector.tensor_tensor(four(heads), four(resid[:, :, :]), at_chunk(beta[:, :], c), ALU.mult))
                u = at_chunk(U[:, :], c)
                last_step()
                step(nc.vector.tensor_copy(u[:, :, :, 0], four(terms[:, 0, :, 0:1])[:, :, :, 0]))
                for t in range(1, C):
                    if c == 0:
                        take_dots(s, DOT_KK[0] + t - 1)
                        dve.wait_ge(att_read_v, s * AV + reads("V", U_DOTS + DOT_KK[0] + t - 1))
                    last_step()
                    step(nc.vector.tensor_tensor(four(terms[:, t, :, 1:t + 1]), nk_row(t, c), u[:, :, :, 0:t], ALU.mult))
                    last_step()
                    step(nc.vector.tensor_reduce(u[:, :, :, t], four(terms[:, t, :, 0:t + 1]), AX.X, ALU.add))
                    if job and t in SOLVE_B:
                        ln_part(job, SOLVE_B[t])
                    if call and t == OUT_STEP:
                        ffn_out(call)
                    if dots and t in TAKE_STEPS:
                        take_dots(s, dots.pop(0))
                last_step()
                nc.vector.transpose(UTr[:, :, :], u.rearrange("p g b t -> p g (b t)")).then_inc(u_turned, 1)
                dve.wait_ge(u_turned, s * CH + (c + 1))
                nc.vector.tensor_tensor(Uz[:, :, :, :], UTr[:, :, :].unsqueeze(2).to_broadcast([P, GP, 2, 32]),
                                        side_ones[:, :].unsqueeze(1).unsqueeze(3).to_broadcast([P, GP, 2, 32]),
                                        ALU.mult).then_inc(u_ready, 1)
                for q in dots:
                    take_dots(s, q)
                beside("d")
                dve.wait_ge(dstate_ready, s * CH + (c + 1))
                step(nc.vector.tensor_tensor(state[:, :, :], state[:, :, :], dstate_ps.rearrange("p (g w) -> p g w", w=32), ALU.add))
                last_step()
                nc.vector.tensor_tensor(state_bd[:, :, :].rearrange("p g (q w) -> p g q w", w=32),
                                        state[:, :, :].unsqueeze(2).to_broadcast([P, GB, QUADS, 32]),
                                        head_ones[:, :].rearrange("p (q w) -> p q w", w=32).unsqueeze(1).to_broadcast([P, GB, QUADS, 32]),
                                        ALU.mult).then_inc(state_ready, 1)
                beside("r")

            def att_out(s, att_job):
                for q in range(DOT_QK[1], DOTS):
                    take_dots(s, q)
                dve.wait_ge(att_step, (s + 1) * ATT_STEPS)
                dve.wait_ge(q_saved, s * CH + CH)
                nc.vector.tensor_tensor(O[:, :], O[:, :], O_in[:, :], ALU.add).then_inc(o_ready, 1)
                if att_job:
                    ln_invert(att_job)
                xs = slab(s)
                for m in range(KT_IN):
                    ps = use(s, U_OUT + m)
                    nc.vector.scalar_tensor_tensor(xs[:, m, :], ps[:, :], p("b_out", m), xs[:, m, :],
                                                   ALU.add, ALU.add).then_inc(att_read_v, 1)
                if att_job:
                    ln_norm(att_job)

            def alone(call, job, second):
                ln_center(job)
                ln_invert(job)
                ln_norm(job)
                if second:
                    for i in range(W_PIECES):
                        convert(i)
                    ln_center(second)
                    ln_invert(second)
                    ln_norm(second)
                ffn_out(call)

            def norm_only(job):
                ln_center(job)
                ln_invert(job)
                ln_norm(job)

            def iteration(s, kind, a, b, jobs):
                first_att, b_job, next_job, att_job = jobs
                if first_att:
                    norm_only(first_att)
                if not a:
                    ln_center(b_job)
                    ln_invert(b_job)
                key_invert(s)
                if not a:
                    ln_norm(b_job)
                key_scale(s)
                if a and b:
                    ln_center(b_job)
                dve.wait_ge(att_read_s, s * AS + 6)

                for c in range(CH):
                    def beside(gap, c=c):
                        for job, parts in ((b_job if a else None, BESIDE_B), (next_job, BESIDE_NEXT), (att_job, BESIDE_ATT)):
                            if job and (c, gap) in parts:
                                ln_part(job, parts[c, gap])
                    chunk(s, c, beside, a if c == OUT_CHUNK and b else None, b_job if c == 0 and a else None)
                att_out(s, att_job)
                ffn_out(b or a)

            run(dve, alone, iteration, norm_only)

        @block.tensor
        def _(pe):
            def ln(part, job):
                i = job[0]
                if part == "mean":
                    pe.wait_ge(ln_summed, i * 1 + 1)
                    if not is_zero(i):
                        pe.wait_ge(ln_read, i * 2)
                if part == "var":
                    pe.wait_ge(ln_sq_summed, i * 1 + 1)
                if part in ("mean", "var"):
                    nc.tensor.matmul(ln_bank[:, :], average[:, :], feature_sum, start=True, stop=True).then_inc(ln_filled, 1)

            def bank_free(call, j):
                n, _, _ = call
                i = j - FFN_BANKS
                if i >= 0:
                    pe.wait_ge(ffn_read, n * FFN_S + (i + 1))
                elif not is_zero(n):
                    if i + FFN_V >= 0:
                        pe.wait_ge(ffn_added, n * FFN_V + (i + 1))
                    else:
                        pe.wait_ge(ffn_read, n * FFN_S + (i + FFN_V + 1))

            def ffn(call, k, starting=False):
                n, off, _ = call

                def loaded(name):
                    if starting:
                        pe.wait_ge(w_ready, W_DONE[name])

                if k < L2:
                    m, up = divmod(k, 2)
                    if k == 0:
                        loaded("w2")
                        pe.wait_ge(ln_lo, n * 1 + 1)
                    bank_free(call, k)
                    name = "w2" if up else "w1"
                    for kk in range(KT_IN):
                        for part, v in enumerate((xn_hi, xn_lo)):
                            mm = nc.tensor.matmul(ffn_ps(off, k), weight(name, kk, m), v[:, kk, :],
                                                  start=kk == 0 and part == 0, stop=kk == KT_IN - 1 and part == 1)
                    mm.then_inc(ffn_filled, 1)
                    return
                layer, name = (0, "h1") if k < L3 else (1, "h2") if k < LO else (2, "w3")
                pair, kk = divmod(k - (L2, L3, LO)[layer], KT_FF)
                if kk == 0:
                    if pair == 0:
                        loaded(name)
                    for i in range(2):
                        bank_free(call, 2 * KT_FF + layer * KT_FF + 2 * pair + i)
                if pair == 0:
                    pe.wait_ge(hid_lo_ready, n * UNITS + (layer * KT_FF + kk + 1))
                for i in range(2):
                    j = 2 * KT_FF + layer * KT_FF + 2 * pair + i
                    for part, v in enumerate((hid_hi[layer % 2], hid_lo[layer % 2])):
                        mm = nc.tensor.matmul(ffn_ps(off, j), weight(name, kk, 2 * pair + i), v[:, kk, :],
                                              start=kk == 0 and part == 0, stop=kk == KT_FF - 1 and part == 1)
                    if kk == KT_FF - 1:
                        mm.then_inc(ffn_filled, 1)

            def att_use(s, j):
                i = j - ATT_BANKS
                if i >= 0:
                    if ATT_USES[i] == "V":
                        pe.wait_ge(att_read_v, s * AV + reads("V", i))
                    else:
                        pe.wait_ge(att_read_s, s * AS + reads("S", i))
                elif not is_zero(s):
                    pe.wait_ge(att_read_v, s * AV + (i + 1))
                return att_bank[j % ATT_BANKS]

            def project(s, i):
                ps, j = att_use(s, U_PROJ[i]), PROJ[i]
                for k in range(KT_IN):
                    mm = nc.tensor.matmul(ps[:, :], wqkvb_sb[:, k, j * P:(j + 1) * P], xn[:, k, :], start=k == 0, stop=k == KT_IN - 1)
                mm.then_inc(att_filled, 1)

            def dots(s, q):
                pe.wait_ge(pairs_ready, s * DOTS + (q + 1))
                ps, w = att_use(s, U_DOTS + q), HRUNS * dot(q)[3]
                if is_split(q):
                    ones = head_ones16 if dot(q)[0] else head_minus16
                    nc.tensor.matmul(ps[:, 0:w], ones[:, :], pair(pairs_hi, q), start=True, stop=False)
                    nc.tensor.matmul(ps[:, 0:w], ones[:, :], pair(pairs_lo, q), start=False, stop=True).then_inc(att_filled, 1)
                    return
                ones = head_ones if dot(q)[0] else head_minus
                nc.tensor.matmul(ps[:, 0:w], ones[:, :], pair(pairs, q), start=True, stop=True).then_inc(att_filled, 1)

            def retrieve(s, c):
                if c == 0:
                    pe.wait_ge(k_ready, s * KT_IN + KT_IN)
                pe.wait_ge(state_ready, s * CH + (c + 1))
                for g in range(GB):
                    cols = KQ[:, :, :].rearrange("p w (i n) -> p w i n", n=32)[:, :, (g // 2) * CH + c, (g % 2) * C:(g % 2 + 1) * C]
                    mm = nc.tensor.matmul(retr_ps[:, g * 2 * C:(g + 1) * 2 * C], state_bd[:, g, :], cols, start=True, stop=True)
                mm.then_inc(retr_ready, 1)

            def update(s, c):
                pe.wait_ge(kz_ready, s * CH + (c + 1))
                pe.wait_ge(u_ready, s * CH + (c + 1))
                pe.wait_ge(q_saved, s * CH + (c + 1))
                for g in range(GP):
                    mm = nc.tensor.matmul(dstate_ps[:, g * 64:(g + 1) * 64], Kz[:, g, :], Uz[:, g, :, :].rearrange("p b w -> p (b w)"), start=True, stop=True)
                mm.then_inc(dstate_ready, 1)

            def att_out(s):
                pe.wait_ge(o_ready, s * 1 + 1)
                for m in range(KT_IN):
                    ps = att_use(s, U_OUT + m)
                    for k in range(KT_IN):
                        mm = nc.tensor.matmul(ps[:, :], wout_sb[:, k, m * P:(m + 1) * P], O[:, k * N:(k + 1) * N], start=k == 0, stop=k == KT_IN - 1)
                    mm.then_inc(att_filled, 1)

            def attention(s, e):
                for i in range(len(PROJ)):
                    if e == E_PROJ[i]:
                        if i == 0:
                            pe.wait_ge(att_normed, s * KT_IN + KT_IN)
                        project(s, i)
                if e == E_NORM:
                    pe.wait_ge(att_read_s, s * AS + KT_IN)
                    for g in range(KT_IN):
                        ps = att_use(s, U_NORM + g)
                        nc.tensor.matmul(ps[:, :], head_ones[:, :], k_sq[:, g * N:(g + 1) * N], start=True, stop=True).then_inc(att_filled, 1)
                for c in range(CH):
                    if e == E_RETR[c]:
                        retrieve(s, c)
                    if e == E_STATE[c]:
                        update(s, c)
                for q in dots_at(e):
                    dots(s, q)
                if e == E_OUT:
                    att_out(s)

            def alone(call, job, second):
                by_itself(call, job, second, ln, lambda c, k: ffn(c, k, second is not None))

            def iteration(s, kind, a, b, jobs):
                if is_zero(s):
                    pe.wait_ge(att_w_loaded, 32)
                in_order(s, kind, a, b, jobs, attention, ln, ffn)

            pe.wait_ge(masks_ready, 2)
            pe.wait_ge(side_ready, 5)
            run(pe, alone, iteration, lambda job: whole_norm(job, ln))


def kernel(**inputs):
    import numpy as np
    import concourse.bacc as bacc
    from concourse.bass_utils import run_bass_kernel_spmd

    def of(name):
        return np.asarray(inputs["L0_" + name])

    def rows(a):
        return np.ascontiguousarray(a.reshape(-1, P, a.shape[-1]).transpose(1, 0, 2))

    x = of("attn_x").reshape(2, 2, SLABS, CH, C, KT_IN, P)
    x = np.ascontiguousarray(x.transpose(6, 2, 5, 0, 3, 1, 4)).reshape(P, SLABS, KT_IN, N)
    vectors = {"w1_s": "ffn_w1_s", "w2_s": "ffn_w2_s", "h1_s": "ffn_h1_s", "h2_s": "ffn_h2_s", "w3_s": "ffn_w3_s",
               "ln_g": "attn_ln_g", "ln_b": "attn_ln_b", "b_qkvb": "attn_b_qkvb", "b_out": "attn_b_out"}
    weights = {"w1": "ffn_w1_w", "w2": "ffn_w2_w", "h1": "ffn_h1_w", "h2": "ffn_h2_w", "w3": "ffn_w3_w"}
    arrays = {
        "x": x,
        "w": np.ascontiguousarray(np.concatenate([rows(of(weights[n]).T).reshape(P, -1) for n in W_AT], axis=1)),
        "wqkvb": rows(of("attn_w_qkvb")), "wout": rows(of("attn_w_out")),
        "par": np.ascontiguousarray(np.concatenate([of(vectors[n]).reshape(-1, P) for n in PAR]).T),
    }
    nc = bacc.Bacc("TRN2", target_bir_lowering=False, num_devices=1, dynamic_dma_scratch_size=1024)
    args = [nc.dram_tensor(f"in_{n}", list(a.shape), F32, kind="ExternalInput").ap() for n, a in arrays.items()]
    out = nc.dram_tensor("out", list(x.shape), F32, kind="ExternalOutput").ap()
    build(nc, *args, out)
    r = run_bass_kernel_spmd(nc, [{f"in_{n}": a for n, a in arrays.items()}], core_ids=[0])
    y = np.asarray(r.results[0]["out"]).reshape(P, SLABS, KT_IN, 2, CH, 2, C)
    return np.ascontiguousarray(y.transpose(3, 5, 1, 4, 6, 2, 0)).reshape(B, T, HID)
```
